# Optimizing a Trainium2 kernel written in Bass

```python
import numpy as np
import jax
import jax.numpy as jnp

def _softmax(x, axis=-1):
    return jax.nn.softmax(x, axis=axis)

def _gelu(x):
    return jax.nn.gelu(x, approximate=True)

def _silu(x):
    return jax.nn.silu(x)

def _sigmoid(x):
    return jax.nn.sigmoid(x)

def _layernorm(x, axis=-1, eps=1e-05):
    m = jnp.mean(x, axis=axis, keepdims=True)
    v = jnp.var(x, axis=axis, keepdims=True)
    return (x - m) / jnp.sqrt(v + eps)

def _scatter_add(tgt, idx, src, axis=0):
    return tgt.at[idx].add(src)

def _segment_sum(src, seg, n):
    return jax.ops.segment_sum(src, seg, n)
kernel_name = 'mk_adj_preln_d2_adj_r2_9b021c'

def setup_inputs(seed: int=0):
    np.random.seed(seed)
    _w = jnp.asarray

    def _rec_inputs():
        import jax
        import jax.numpy as jnp
        _gk = jax.random.key(seed)
        x = -0.0005207 + 1.001 * jax.random.normal(jax.random.fold_in(_gk, 1), (8192, 128), jnp.float32)
        _a = jax.random.bernoulli(jax.random.fold_in(_gk, 2), 0.00195312, (8192, 8192))
        _a = jnp.logical_or(_a, jnp.swapaxes(_a, -1, -2))
        _a = jnp.logical_or(_a, jnp.eye(8192, dtype=bool))
        adj = _a.astype(jnp.int32)
        return (x, adj)
    x, adj = _rec_inputs()

    def _L0_gnn_setup():
        import jax, jax.numpy as jnp
        import numpy as np
        N = 4096
        F_IN = 128
        F_OUT = 128
        ALPHA = 0.2
        NEG_BIG = -9000000000000000.0
        key = jax.random.key(seed)
        k1, k2, k3, k4 = jax.random.split(key, 4)
        h = jax.random.normal(k1, (N, F_IN), dtype=jnp.float32)
        adj = jax.random.randint(k2, (N, N), 0, 2, dtype=jnp.int32)
        W = jax.random.normal(k3, (F_IN, F_OUT), dtype=jnp.float32) * (1.414 / np.sqrt(F_IN))
        a = jax.random.normal(k4, (2 * F_OUT, 1), dtype=jnp.float32) * (1.414 / np.sqrt(2 * F_OUT))
        return {'h': h, 'adj': adj, 'W': W, 'a': a}
    _L0_gnn_all = _L0_gnn_setup()
    _L0_gnn_in = {k: v for k, v in _L0_gnn_all.items() if k in ('W', 'a')}
    del _L0_gnn_all

    def _L1_gnn_setup():
        import jax, jax.numpy as jnp
        import numpy as np
        N, D, H = (4096, 128, 128)
        KEEP_RATIO = 0.5
        TEMP = 1.0
        COS_EPS = 0.0001
        NEG = -9000000000000000.0

        def _cos_normalize(x):
            n = jnp.linalg.norm(x, axis=-1, keepdims=True)
            return x / jnp.maximum(n, COS_EPS)
        key = jax.random.key(seed)
        k1, k2, k3, k4 = jax.random.split(key, 4)
        features = jax.random.normal(k1, (N, D), dtype=jnp.float32)
        adj = jax.random.randint(k2, (N, N), 0, 2, dtype=jnp.int32)
        Wq = jax.random.normal(k3, (H, D), dtype=jnp.float32) * 0.001
        Wk = jax.random.normal(k4, (H, D), dtype=jnp.float32) * 0.001
        return {'features': features, 'adj': adj, 'Wq': Wq, 'Wk': Wk}
    _L1_gnn_all = _L1_gnn_setup()
    _L1_gnn_in = {k: v for k, v in _L1_gnn_all.items() if k in ('Wq', 'Wk')}
    del _L1_gnn_all
    return {'x': x, 'adj': adj, 'L0_gnn_W': _L0_gnn_in['W'], 'L0_gnn_a': _L0_gnn_in['a'], 'L1_gnn_Wq': _L1_gnn_in['Wq'], 'L1_gnn_Wk': _L1_gnn_in['Wk']}

def reference(x, adj, L0_gnn_W, L0_gnn_a, L1_gnn_Wq, L1_gnn_Wk):
    import jax
    import jax.numpy as jnp

    def _L0_gnn_ref(h, adj, W, a):
        import jax, jax.numpy as jnp
        import numpy as np
        N = 4096
        F_IN = 128
        F_OUT = 128
        ALPHA = 0.2
        NEG_BIG = -9000000000000000.0
        wh = h @ W
        wh1 = wh @ a[:F_OUT, :]
        wh2 = wh @ a[F_OUT:, :]
        e = wh1 + wh2.T
        e = jnp.where(e > 0, e, ALPHA * e)
        e = jnp.where(adj > 0, e, NEG_BIG)
        attention = jax.nn.softmax(e, axis=-1)
        h_prime = attention @ wh
        return jax.nn.elu(h_prime)

    def _L1_gnn_ref(features, adj, Wq, Wk):
        import jax, jax.numpy as jnp
        import numpy as np
        N, D, H = (4096, 128, 128)
        KEEP_RATIO = 0.5
        TEMP = 1.0
        COS_EPS = 0.0001
        NEG = -9000000000000000.0

        def _cos_normalize(x):
            n = jnp.linalg.norm(x, axis=-1, keepdims=True)
            return x / jnp.maximum(n, COS_EPS)
        Qn = _cos_normalize(features @ Wq.T)
        Kn = _cos_normalize(features @ Wk.T)
        raw_att = Kn @ Qn.T
        att = jnp.where(adj > 0, raw_att, NEG) * TEMP
        att = jax.nn.softmax(att, axis=1)
        prop_fea = att @ features
        adj_mask = (jnp.sum(adj, axis=1) > 0).astype(features.dtype)[:, None]
        prop_fea = adj_mask * prop_fea + (1.0 - adj_mask) * features
        return (1.0 - KEEP_RATIO) * prop_fea + KEEP_RATIO * features
    h = jnp.maximum(_layernorm(x, axis=-1), 0.0)
    x = x + _L0_gnn_ref(h, adj, L0_gnn_W, L0_gnn_a)
    h = jnp.maximum(_layernorm(x, axis=-1), 0.0)
    x = x + _L1_gnn_ref(h, adj, L1_gnn_Wq, L1_gnn_Wk)
    return x

_drawn_inputs = setup_inputs


def setup_inputs(seed=0):
    import zlib

    import numpy as np

    out = dict(_drawn_inputs(seed))
    spreads = {}
    factors = {}
    for name, (base, spread) in spreads.items():
        noise = np.random.default_rng([zlib.crc32(name.encode()), seed]).standard_normal(out[name].shape)
        drawn = base * np.exp(spread * noise) if base else spread * noise
        out[name] = jnp.asarray(drawn.astype(out[name].dtype))
    for name, factor in factors.items():
        out[name] = (out[name] * factor).astype(out[name].dtype)
    return out
```

```python
import numpy as np
import concourse.bass as bass
from concourse import mybir
from contextlib import ExitStack

F32, F16, I32 = mybir.dt.float32, mybir.dt.float16, mybir.dt.int32
ALU = mybir.AluOpType
ACT = mybir.ActivationFunctionType
AX = mybir.AxisListType

N, D, P = 8192, 128, 128
T = N // P
IW = 512
NI = N // IW
NJ = T // 2
STEP = 2048
RING = 4
C0 = 1024
NC0 = N // C0
IT0 = C0 // P
G0 = T // (STEP // C0) // RING
IT1 = IW // P
G1 = T // (STEP // IW) // RING
VW = D + 2
UW = 2 * D + 2
EPS = 1e-5
ALPHA = 0.2
LIFT = 30.0
EMPTY = 1e-36
COS_EPS = 1e-4
UNIT = 64.0
TINY = 1e-30
LN = ("diff", "total", "m2", "dsq", "between", "var", "rstd", "nbias")
EPI0 = ("den", "neg", "elu", "x1", "stats") + LN + ("hi", "lo")
EPI1 = ("some", "max", "recip", "scale", "keep", "kept", "y")


def graph_layers(nc, x, adj, w, wt, a, wqk, out):
    ctx = ExitStack()
    with ctx:
        def sb(name, shape, dt=F32):
            return ctx.enter_context(nc.sbuf_tensor(name, shape, dt))

        def sem(name):
            return ctx.enter_context(nc.semaphore(name))

        a_rows = nc.dram_tensor("a_rows", [T, P], F32, kind="Internal").ap()
        x1_dram = nc.dram_tensor("x1_dram", [P, N], F32, kind="Internal").ap()
        h_dram = nc.dram_tensor("h_dram", [P, N], F32, kind="Internal").ap()

        ident = sb("ident", [P, P])
        w_ext = sb("w_ext", [P, VW])
        wt_sb = sb("wt_sb", [P, P])
        a_sb = sb("a_sb", [P, 2])
        wqk_sb = sb("wqk_sb", [P, 2 * D])
        empty_w = sb("empty_w", [P, P])
        v_sum = sb("v_sum", [P, D + 1])
        stats = sb("stats", [P, T, 6])
        small = sb("small", [P, 6, T])
        rstd = sb("rstd", [P, T])
        nbias = sb("nbias", [P, T])
        ab_col = sb("ab_col", [P, 2, T])
        ab_max = sb("ab_max", [P, 2])
        ab_top = sb("ab_top", [P, 2])
        shift = sb("shift", [P, 6])
        f_col = sb("f_col", [P, T])
        s_col = sb("s_col", [P, T])
        ns_col = sb("ns_col", [P, T])
        at_sb = sb("at_sb", [T, P])
        den = sb("den", [P, 4, IT0])
        norm = sb("norm", [P, 4, 8])

        adj_ring = sb("adj_ring", [P, RING, STEP], I32)
        p_ring = sb("p_ring", [P, RING, STEP])
        r_ring = sb("r_ring", [P, 2, C0])
        v_buf = sb("v_buf", [P, T * VW])
        q_buf = sb("q_buf", [P, 2, N], F16)
        u_buf = sb("u_buf", [P, T, UW], F16)
        hl_buf = sb("hl_buf", [P, 2, 2, STEP], F16)

        v0 = v_buf[:, :].rearrange("p (t c) -> p t c", c=VW)
        k_buf = v_buf[:, 0:N].bitcast(F16).rearrange("p (s n) -> p s n", s=2)
        xs = q_buf[:, :, :].rearrange("p s n -> p (s n)").bitcast(F32)
        scratch = hl_buf[:, :, :, :].rearrange("p s r n -> p (s r n)").bitcast(F32)
        z_buf = scratch[:, 0:C0]
        e_buf = scratch[:, C0:2 * C0]
        h_buf = scratch[:, 2 * C0:3 * C0]
        flat = p_ring[:, :, :].rearrange("p r n -> p (r n)")
        h_ring = flat[:, 0:2 * IW].rearrange("p (r n) -> p r n", r=2)
        ht_ring = flat[:, 2 * IW:4 * IW].rearrange("p (r n) -> p r n", r=2)
        sq_buf = flat[:, 4 * IW:6 * IW]
        qk_ring = flat[:, 6 * IW:10 * IW].rearrange("p (r n) -> p r n", r=2)
        e_x1 = r_ring[:, 0, 0:IW]
        e_h = r_ring[:, 0, IW:2 * IW]
        e_t = r_ring[:, 1, 0:IW]
        e_y = r_ring[:, 1, IW:2 * IW]

        bank = ctx.enter_context(nc.psum_tensor("bank", [P, 8, 512], F32))

        s_w = sem("weights_in")
        s_x = [sem(f"x_in{i}") for i in range(4)]
        s_ident = sem("ident_ready")
        s_const = sem("const_ready")
        s_wa = sem("wa_ready")
        s_wa_sb = sem("wa_copied")
        s_stats = sem("ln1_statistics")
        s_stat = sem("ln1_step")
        s_sd = sem("ln1_root")
        s_h1 = sem("h1_ready")
        s_h1t = sem("h1t_ready")
        s_h1c = sem("h1t_copied")
        s_wh = sem("wh_ready")
        s_whc = sem("wh_copied")
        s_ab = sem("ab_step")
        s_top = sem("ab_top_ready")
        s_exp0 = sem("factors_ready")
        s_at = sem("a_transposed")
        s_atc = sem("a_rows_copied")
        s_aw = sem("a_rows_written")
        s_rin = [sem("r_in0"), sem("r_in1")]
        s_r = sem("r_ready")
        s_vsum = sem("v_sum_ready")
        s_adj = [sem(f"adj_in{k}") for k in range(RING)]
        s_half = sem("relu_half")
        s_odd = sem("odd_tile_ready")
        s_even = sem("even_tile_ready")
        s_p = sem("weights_ready")
        s_used = sem("weights_used")
        s_acc = sem("layer0_sums_ready")
        s_free = sem("layer0_sums_read")
        s_ev = sem("epilogue0_vector")
        s_ea = sem("epilogue0_scalar")
        s_x1w = sem("x1_written")
        s_hw = sem("h_written")
        s_hm = [sem("h_in0"), sem("h_in1")]
        s_ht = sem("ht_ready")
        s_htc = sem("ht_copied")
        s_qk = sem("qk_ready")
        s_sq = sem("squares_ready")
        s_n2 = sem("norm_step")
        s_nr = sem("norm_root")
        s_qn = sem("qk_scaled")
        s_qt = sem("qkt_ready")
        s_hi = sem("qk_high")
        s_lo = sem("qk_low")
        s_s = sem("scores_ready")
        s_e = sem("exp_ready")
        s_m = sem("masked")
        s_ph = sem("high_ready")
        s_pl = sem("low_ready")
        s_pv = sem("layer1_used")
        s_o = sem("layer1_sums_ready")
        s_ofree = sem("layer1_sums_read")
        s_fv = sem("epilogue1_vector")
        s_fin = sem("residual_in")
        s_out = sem("out_written")

        block = ctx.enter_context(nc.Block())

        def acc0(par, it):
            b, k = 3 * par + it // 3, it % 3
            return bank[:, b, k * (D + 1):(k + 1) * (D + 1)]

        def acc0_group(par, b):
            n = min(3, IT0 - 3 * b)
            return bank[:, 3 * par + b, 0:n * (D + 1)].rearrange("p (n c) -> p n c", n=n)

        def acc1(par, it):
            return bank[:, 4 + 2 * par + it // 2, (it % 2) * (D + 1):(it % 2 + 1) * (D + 1)]

        def p0(k):
            return p_ring[:, k, :].rearrange("p (b j n) -> p b j n", b=2, j=2)

        def chunks0(eng, chunk):
            chunk(0, 0)
            with eng.Fori(0, (NC0 - 2) // 2) as pair:
                chunk(2 * pair + 1, 1)
                chunk(2 * pair + 2, 0)
            chunk(NC0 - 1, 1)

        def chunks1(eng, chunk):
            chunk(0, 0)
            with eng.Fori(0, (NI - 2) // 2) as pair:
                chunk(2 * pair + 1, 1)
                chunk(2 * pair + 2, 0)
            chunk(NI - 1, 1)

        SN0 = NC0 * G0

        @block.sync
        def _(sp):
            for i in range(4):
                q = slice(i * N // 4, (i + 1) * N // 4)
                sp.dma_start(xs[:, q], x[:, q]).then_inc(s_x[i], 16)
            sp.dma_start(w_ext[:, 0:D], w).then_inc(s_w, 16)
            sp.dma_start(wt_sb[:, :], wt).then_inc(s_w, 16)
            sp.dma_start(a_sb[:, :], a).then_inc(s_w, 16)
            sp.dma_start(wqk_sb[:, :], wqk).then_inc(s_w, 16)

            adj_lanes = adj.rearrange("b j p n -> p b j n")

            def load0(c, j, k):
                sp.dma_start(adj_ring[:, k, :].rearrange("p (b j n) -> p b j n", b=2, j=1),
                             adj_lanes[:, bass.ds(2 * c, 2), bass.ds(j, 1), :]).then_inc(s_adj[k], 16)

            def load1(i, j, k):
                sp.dma_start(adj_ring[:, k, :].rearrange("p (b j n) -> p b j n", b=1, j=2),
                             adj_lanes[:, bass.ds(i, 1), bass.ds(2 * j, 2), :]).then_inc(s_adj[k], 16)

            for k in range(RING):
                load0(0, k, k)
            sp.wait_ge(s_atc, 1)
            sp.dma_start(a_rows[:, :], at_sb[:, :]).then_inc(s_aw, 16)
            sp.wait_ge(s_aw, 16)
            a_flat = a_rows.rearrange("t p -> (t p)")

            def load_r(c, par):
                row = a_flat[bass.ds(c * C0, C0)].rearrange("(o n) -> o n", o=1)
                sp.dma_start(r_ring[:, par, :], row.to_broadcast([P, C0])).then_inc(s_rin[par], 16)

            load_r(0, 0)

            def chunk(c, par):
                first = isinstance(c, int) and c == 0
                last = isinstance(c, int) and c == NC0 - 1

                def group(g):
                    for k in range(RING):
                        sp.wait_ge(s_p, RING * (G0 * c + g - 1) + k + 1)
                        load0(c, RING * g + k, k)

                if not first:
                    group(0)
                if not last:
                    if not first:
                        sp.wait_ge(s_p, RING * G0 * c)
                    load_r(c + 1, 1 - par)
                with sp.Fori(1, G0) as g:
                    group(g)

            chunks0(sp, chunk)

            act_h_writes = NC0
            sp.wait_ge(s_hw, 16 * act_h_writes)

            def load_h(g, r):
                sp.dma_start(h_ring[:, r, :], h_dram[:, bass.ds(g * IW, IW)]).then_inc(s_hm[r], 16)

            sp.wait_ge(s_used, RING * SN0)
            load_h(0, 0)
            load_h(1, 1)
            for k in range(RING):
                load1(0, k, k)
            with sp.Fori(1, NI // 2) as gg:
                for r in range(2):
                    sp.wait_ge(s_ht, 2 * (gg - 1) + r + 1)
                    load_h(2 * gg + r, r)

            def chunk1(i, par):
                first = isinstance(i, int) and i == 0

                def group(g):
                    for k in range(RING):
                        sp.wait_ge(s_m, RING * (G1 * i + g - 1) + k + 1)
                        load1(i, RING * g + k, k)

                if not first:
                    group(0)
                with sp.Fori(1, G1) as g:
                    group(g)

            chunks1(sp, chunk1)

        @block.gpsimd
        def _(pool):
            nc.gpsimd.memset(ident[:, :], 0.0).then_inc(s_ident, 1)
            pool.wait_ge(s_ident, 1)
            nc.gpsimd.affine_select(out=ident[:, :], in_=ident[:, :], compare_op=ALU.not_equal, fill=1.0,
                                    base=0, pattern=[[-1, P]], channel_multiplier=1).then_inc(s_ident, 1)
            nc.gpsimd.memset(empty_w[:, :], EMPTY).then_inc(s_const, 1)
            nc.gpsimd.memset(u_buf[:, :, D:D + 2], 1.0).then_inc(s_const, 1)
            pool.wait_ge(s_ab, 4)
            nc.gpsimd.partition_all_reduce(ab_top[:, :], ab_max[:, :], P, bass.bass_isa.ReduceOp.max).then_inc(s_top, 1)

        @block.scalar
        def _(act):
            act.wait_ge(s_wa, 1)
            nc.scalar.activation(w_ext[:, D:VW], bank[:, 7, 0:2], ACT.Copy).then_inc(s_wa_sb, 1)
            act.wait_ge(s_stat, LN.index("var") + 1)
            nc.scalar.activation(small[:, 4, :], small[:, 3, :], ACT.Sqrt).then_inc(s_sd, 1)
            act.wait_ge(s_stat, len(LN))

            def norm1(g, r):
                act.nop(nofuse=True)
                for k in range(4):
                    t = 4 * g + k
                    ins = nc.scalar.activation(h_ring[:, r, k * P:(k + 1) * P], xs[:, bass.ds(t * P, P)], ACT.Relu,
                                               bias=nbias[:, bass.ds(t, 1)], scale=rstd[:, bass.ds(t, 1)])
                ins.then_inc(s_h1, 1)

            def evac1(g, r):
                act.wait_ge(s_wh, g + 1)
                act.nop(nofuse=True)
                for b in range(2):
                    src = bank[:, 2 + 2 * r + b, 0:2 * VW].rearrange("p (n c) -> p n c", n=2)
                    ins = nc.scalar.activation(v0[:, bass.ds(4 * g + 2 * b, 2), :], src, ACT.Copy)
                ins.then_inc(s_whc, 1)

            norm1(0, 0)
            norm1(1, 1)
            evac1(0, 0)
            with act.Fori(1, T // 8) as gg:
                for r in range(2):
                    act.wait_ge(s_h1t, 2 * gg + r - 1)
                    norm1(2 * gg + r, r)
                    evac1(2 * gg + r - 1, 1 - r)
            evac1(T // 4 - 1, 1)

            act.wait_ge(s_at, 1)
            nc.scalar.activation(at_sb[:, :], bank[0:T, 6, 0:P], ACT.Copy).then_inc(s_atc, 1)
            act.wait_ge(s_ab, 12)
            nc.scalar.activation(f_col[:, :], ab_col[:, 1, :], ACT.Exp, bias=shift[:, 2:3]).then_inc(s_exp0, 1)
            nc.scalar.activation(s_col[:, :], ab_col[:, 1, :], ACT.Exp, bias=shift[:, 3:4], scale=ALPHA).then_inc(s_exp0, 1)
            act.wait_ge(s_exp0, 2)
            nc.scalar.activation(ns_col[:, :], s_col[:, :], ACT.Copy, scale=-1.0).then_inc(s_exp0, 1)
            act.wait_ge(s_exp0, 3)

            def row_factor(c, par):
                act.wait_ge(s_rin[par], 16 * ((c - par) // 2 + 1) if isinstance(c, int) else 8 * (c - par) + 16)
                nc.scalar.activation(r_ring[:, par, :], r_ring[:, par, :], ACT.Exp, bias=shift[:, 4:5],
                                     scale=1.0 - ALPHA).then_inc(s_r, 1)

            row_factor(0, 0)

            def epilogue(c, par):
                at = lambda step: len(EPI0) * c + EPI0.index(step) + 1
                act.wait_ge(s_ev, at("den"))
                for it in range(IT0):
                    ins = nc.scalar.activation(z_buf[:, it * P:(it + 1) * P], acc0(par, it)[:, 0:D], ACT.Copy,
                                               scale=den[:, 0, it:it + 1])
                ins.then_inc(s_free, 1)
                act.wait_ge(s_ev, at("neg"))
                nc.scalar.activation(e_buf, e_buf, ACT.Exp).then_inc(s_ea, 1)
                act.wait_ge(s_ev, at("x1"))
                act.dma_start(x1_dram[:, bass.ds(c * C0, C0)], xs[:, bass.ds(c * C0, C0)]).then_inc(s_x1w, 16)
                act.wait_ge(s_ev, at("var"))
                nc.scalar.activation(small[:, 4, 0:IT0], small[:, 3, 0:IT0], ACT.Sqrt).then_inc(s_ea, 1)
                act.wait_ge(s_ev, at("nbias"))
                if not (isinstance(c, int) and c == 0):
                    act.wait_ge(s_hw, 16 * c)
                act.nop(nofuse=True)
                for it in range(IT0):
                    ins = nc.scalar.activation(h_buf[:, it * P:(it + 1) * P], xs[:, bass.ds(c * C0 + it * P, P)],
                                               ACT.Relu, bias=nbias[:, it:it + 1], scale=rstd[:, it:it + 1])
                ins.then_inc(s_ea, 1)
                act.wait_ge(s_ea, 3 * c + 3)
                act.dma_start(h_dram[:, bass.ds(c * C0, C0)], h_buf).then_inc(s_hw, 16)

            def chunk(c, par):
                first = isinstance(c, int) and c == 0
                last = isinstance(c, int) and c == NC0 - 1

                def group(g, peeled=False):
                    for k in range(RING):
                        n = RING * (G0 * c + g) + k
                        j = 2 * (RING * g + k) + 1
                        if not (first and peeled):
                            act.wait_ge(s_used, n - RING + 1)
                            act.nop(nofuse=True)
                        dst = p0(k)[:, :, 1, :]
                        row = r_ring[:, par, :].rearrange("p (b n) -> p b n", b=2)
                        nc.scalar.activation(dst, row, ACT.Relu, bias=ns_col[:, bass.ds(j, 1)],
                                             scale=f_col[:, bass.ds(j, 1)]).then_inc(s_half, 1)
                        act.wait_ge(s_half, n + 1)
                        act.nop(nofuse=True)
                        nc.scalar.activation(dst, dst, ACT.Identity, bias=s_col[:, bass.ds(j, 1)]).then_inc(s_odd, 1)

                if first:
                    act.wait_ge(s_r, 1)
                else:
                    act.wait_ge(s_r, c + 1)
                group(0, peeled=True)
                if not first:
                    epilogue(c - 1, 1 - par)
                if not last:
                    row_factor(c + 1, 1 - par)
                with act.Fori(1, G0) as g:
                    group(g)

            chunks0(act, chunk)
            epilogue(NC0 - 1, 1)

            act.wait_ge(s_x1w, 16 * NC0)

            def copy_ht(g, r):
                act.wait_ge(s_ht, g + 1)
                nc.scalar.activation(ht_ring[:, r, :], bank[:, r, :], ACT.Copy).then_inc(s_htc, 1)

            def square(g, r):
                act.wait_ge(s_qk, g + 1)
                nc.scalar.activation(sq_buf, bank[:, 2 + 2 * r:4 + 2 * r, :].rearrange("p b n -> p (b n)"),
                                     ACT.Square).then_inc(s_sq, 1)

            def high(g):
                act.wait_ge(s_qt, g + 1)
                act.nop(nofuse=True)
                nc.scalar.activation(q_buf[:, 0, bass.ds(g * IW, IW)], bank[:, 6, :], ACT.Copy).then_inc(s_hi, 1)
                nc.scalar.activation(k_buf[:, 0, bass.ds(g * IW, IW)], bank[:, 7, :], ACT.Copy).then_inc(s_hi, 1)

            def root(g):
                act.wait_ge(s_n2, 3 * g + 1)
                nc.scalar.activation(norm[:, 1, :], norm[:, 0, :], ACT.Sqrt).then_inc(s_nr, 1)

            copy_ht(0, 0)
            copy_ht(1, 1)
            square(0, 0)
            root(0)
            with act.Fori(0, NI // 2 - 1) as gg:
                for r in range(2):
                    g = 2 * gg + r + 1
                    copy_ht(g + 1, r)
                    act.wait_ge(s_n2, 3 * (g - 1) + 1)
                    square(g, 1 - r)
                    high(g - 1)
                    root(g)
            act.wait_ge(s_n2, 3 * (NI - 2) + 1)
            square(NI - 1, 1)
            high(NI - 2)
            root(NI - 1)
            high(NI - 1)

            def exps(n, k, start):
                for hf in range(2):
                    act.wait_ge(s_s, 2 * n + hf + 1)
                    if not start:
                        act.wait_ge(s_pl, n - RING + 1)
                    nc.scalar.activation(p_ring[:, k, hf * 1024:(hf + 1) * 1024],
                                         bank[:, 2 * hf:2 * hf + 2, :].rearrange("p b n -> p (b n)"), ACT.Exp,
                                         scale=1.0 / (UNIT * UNIT)).then_inc(s_e, 1)

            def high_part(n, k, start):
                act.wait_ge(s_m, n + 1)
                if not start:
                    act.wait_ge(s_pv, n - 1)
                nc.scalar.activation(hl_buf[:, 0, k % 2, :], p_ring[:, k, :], ACT.Copy).then_inc(s_ph, 1)

            def epilogue1(i, par):
                at = lambda step: len(EPI1) * i + EPI1.index(step) + 1
                act.wait_ge(s_fv, at("scale"))
                for it in range(IT1):
                    ins = nc.scalar.activation(e_t[:, it * P:(it + 1) * P], acc1(par, it)[:, 0:D], ACT.Copy,
                                               scale=den[:, 3, it:it + 1])
                ins.then_inc(s_ofree, 1)
                act.wait_ge(s_fv, at("y"))
                act.dma_start(out[:, bass.ds(i * IW, IW)], e_y).then_inc(s_out, 16)

            def residual(i):
                act.dma_start(e_x1, x1_dram[:, bass.ds(i * IW, IW)]).then_inc(s_fin, 16)
                act.dma_start(e_h, h_dram[:, bass.ds(i * IW, IW)]).then_inc(s_fin, 16)

            def chunk1(i, par):
                first = isinstance(i, int) and i == 0

                def group(g, peeled=False):
                    for k in range(RING):
                        n = RING * (G1 * i + g) + k
                        start = first and peeled
                        exps(n, k, start)
                        if not (start and k == 0):
                            high_part(n - 1, (k - 1) % RING, start and k < 3)

                group(0, peeled=True)
                if not first:
                    epilogue1(i - 1, 1 - par)
                    residual(i)
                with act.Fori(1, G1) as g:
                    group(g)

            act.wait_ge(s_hw, 16 * NC0)
            residual(0)
            chunks1(act, chunk1)
            high_part(NI * RING * G1 - 1, RING - 1, False)
            epilogue1(NI - 1, 1)
            act.wait_ge(s_out, 16 * NI)

        @block.vector
        def _(dve):
            V = nc.vector

            def layer_norm(cols, root_ready, at, done):
                me, mo = stats[:, 0:cols, 1], stats[:, 0:cols, 4]
                qe, qo = stats[:, 0:cols, 2], stats[:, 0:cols, 5]
                diff, total, sq, var = (small[:, i, 0:cols] for i in range(4))
                V.tensor_tensor(diff, me, mo, ALU.subtract).then_inc(done, 1)
                V.tensor_tensor(total, me, mo, ALU.add).then_inc(done, 1)
                V.tensor_tensor(sq, qe, qo, ALU.add).then_inc(done, 1)
                dve.wait_ge(done, at("m2"))
                V.tensor_tensor(var, diff, diff, ALU.mult).then_inc(done, 1)
                dve.wait_ge(done, at("dsq"))
                V.tensor_scalar(var, var, 0.25, EPS, ALU.mult, ALU.add).then_inc(done, 1)
                dve.wait_ge(done, at("between"))
                V.scalar_tensor_tensor(var, sq, 1.0 / D, var, ALU.mult, ALU.add).then_inc(done, 1)
                dve.wait_ge(*root_ready)
                V.reciprocal(rstd[:, 0:cols], small[:, 4, 0:cols]).then_inc(done, 1)
                dve.wait_ge(done, at("rstd"))
                V.scalar_tensor_tensor(nbias[:, 0:cols], total, -0.5, rstd[:, 0:cols],
                                       ALU.mult, ALU.mult).then_inc(done, 1)

            for i in range(4):
                dve.wait_ge(s_x[i], 16)
                with dve.Fori(4 * i, 4 * i + 4) as g:
                    for k in range(4):
                        t = 4 * g + k
                        ins = V.bn_stats(stats[:, bass.ds(t, 1), :].rearrange("p o s -> p (o s)"),
                                         xs[:, bass.ds(t * P, P)])
                    ins.then_inc(s_stats, 1)
            dve.wait_ge(s_stats, T // 4)
            layer_norm(T, (s_sd, 1), lambda step: LN.index(step) + 1, s_stat)

            def copy_h1t(g, r):
                dve.wait_ge(s_h1t, g + 1)
                V.tensor_copy(ht_ring[:, r, :], bank[:, r, :]).then_inc(s_h1c, 1)

            copy_h1t(0, 0)
            copy_h1t(1, 1)
            with dve.Fori(1, T // 8) as gg:
                for r in range(2):
                    dve.wait_ge(s_wh, 2 * gg + r - 1)
                    copy_h1t(2 * gg + r, r)

            dve.wait_ge(s_whc, T // 4)
            V.tensor_copy(ab_col[:, 0, :], v0[:, :, D]).then_inc(s_ab, 1)
            V.tensor_copy(ab_col[:, 1, :], v0[:, :, D + 1]).then_inc(s_ab, 1)
            dve.wait_ge(s_ab, 2)
            V.reduce_max(ab_max[:, 0:1], ab_col[:, 0, :], AX.X).then_inc(s_ab, 1)
            V.reduce_max(ab_max[:, 1:2], ab_col[:, 1, :], AX.X).then_inc(s_ab, 1)
            V.memset(v0[:, :, D], 1.0).then_inc(s_ab, 1)
            dve.wait_ge(s_top, 1)
            top_a, top_b = ab_top[:, 0:1], ab_top[:, 1:2]
            V.tensor_tensor(shift[:, 0:1], top_a, top_b, ALU.add).then_inc(s_ab, 1)
            V.tensor_scalar(shift[:, 2:3], top_b, -1.0, LIFT, ALU.mult, ALU.add).then_inc(s_ab, 1)
            V.tensor_scalar(shift[:, 3:4], top_b, -ALPHA, 2 * LIFT, ALU.mult, ALU.add).then_inc(s_ab, 1)
            V.tensor_scalar(shift[:, 4:5], top_b, 1.0 - ALPHA, LIFT, ALU.mult, ALU.add).then_inc(s_ab, 1)
            dve.wait_ge(s_ab, 9)
            V.tensor_scalar(shift[:, 1:2], shift[:, 0:1], 1.0 - ALPHA, 0.0, ALU.mult, ALU.max).then_inc(s_ab, 1)
            dve.wait_ge(s_ab, 10)
            V.tensor_tensor(shift[:, 3:4], shift[:, 3:4], shift[:, 1:2], ALU.subtract).then_inc(s_ab, 1)
            V.tensor_tensor(shift[:, 4:5], shift[:, 4:5], shift[:, 1:2], ALU.subtract).then_inc(s_ab, 1)

            def epilogue(c, par):
                at = lambda step: len(EPI0) * c + EPI0.index(step) + 1
                dve.wait_ge(s_acc, c + 1)
                for b in range(3):
                    g = acc0_group(par, b)
                    ins = V.reciprocal(den[:, 0, 3 * b:3 * b + g.shape[1]], g[:, :, D])
                ins.then_inc(s_ev, 1)
                dve.wait_ge(s_free, c + 1)
                V.tensor_scalar(e_buf, z_buf, 0.0, None, ALU.min).then_inc(s_ev, 1)
                dve.wait_ge(s_ea, 3 * c + 1)
                V.scalar_tensor_tensor(z_buf, z_buf, 0.0, e_buf, ALU.max, ALU.add).then_inc(s_ev, 1)
                dve.wait_ge(s_ev, at("elu"))
                x1 = xs[:, bass.ds(c * C0, C0)]
                V.scalar_tensor_tensor(x1, z_buf, -1.0, x1, ALU.add, ALU.add).then_inc(s_ev, 1)
                dve.wait_ge(s_ev, at("x1"))
                dve.nop(nofuse=True)
                for it in range(IT0):
                    ins = V.bn_stats(stats[:, it, :], xs[:, bass.ds(c * C0 + it * P, P)])
                ins.then_inc(s_ev, 1)
                dve.wait_ge(s_ev, at("stats"))
                layer_norm(IT0, (s_ea, 3 * c + 2), at, s_ev)
                dve.wait_ge(s_ea, 3 * c + 3)
                h8 = h_buf.rearrange("p (t f) -> p t f", f=D)
                hi = u_buf[:, bass.ds(c * IT0, IT0), 0:D]
                V.tensor_copy(hi, h8).then_inc(s_ev, 1)
                dve.wait_ge(s_ev, at("hi"))
                V.tensor_tensor(u_buf[:, bass.ds(c * IT0, IT0), D + 2:UW], h8, hi, ALU.subtract).then_inc(s_ev, 1)

            def chunk(c, par):
                first = isinstance(c, int) and c == 0

                def group(g, peeled=False):
                    for k in range(RING):
                        turn = G0 * c + g
                        n = RING * turn + k
                        j = 2 * (RING * g + k)
                        if not (first and peeled):
                            dve.wait_ge(s_used, n - RING + 1)
                        row = r_ring[:, par, :].rearrange("p (b n) -> p b n", b=2)
                        V.tensor_scalar(p0(k)[:, :, 0, :], row, f_col[:, bass.ds(j, 1)], s_col[:, bass.ds(j, 1)],
                                        ALU.mult, ALU.max).then_inc(s_even, 1)
                        dve.wait_ge(s_even, n + 1)
                        dve.wait_ge(s_odd, n + 1)
                        dve.wait_ge(s_adj[k], 16 * (turn + 1))
                        V.scalar_tensor_tensor(p_ring[:, k, :], adj_ring[:, k, :], 0.0, p_ring[:, k, :],
                                               ALU.is_gt, ALU.mult).then_inc(s_p, 1)

                dve.wait_ge(s_r, c + 1)
                if first:
                    dve.wait_ge(s_exp0, 3)
                group(0, peeled=True)
                if first:
                    V.reduce_sum(v_sum[:, :], v0[:, :, 0:D + 1].rearrange("p t c -> p c t"), AX.X).then_inc(s_vsum, 1)
                else:
                    epilogue(c - 1, 1 - par)
                with dve.Fori(1, G0) as g:
                    group(g)

            chunks0(dve, chunk)
            epilogue(NC0 - 1, 1)

            def norms(g, r):
                dve.wait_ge(s_sq, g + 1)
                V.reduce_sum(norm[:, 0, :], sq_buf.rearrange("p (v f) -> p v f", f=D), AX.X).then_inc(s_n2, 1)

            def scaled(g, r):
                dve.wait_ge(s_nr, g + 1)
                V.tensor_scalar(norm[:, 2, :], norm[:, 1, :], COS_EPS, 1.0 / UNIT, ALU.max, ALU.mult).then_inc(s_n2, 1)
                dve.wait_ge(s_n2, 3 * g + 2)
                V.reciprocal(norm[:, 3, :], norm[:, 2, :]).then_inc(s_n2, 1)
                dve.wait_ge(s_n2, 3 * g + 3)
                src = bank[:, 2 + 2 * r:4 + 2 * r, :].rearrange("p b n -> p (b n)").rearrange("p (v f) -> p v f", f=D)
                V.tensor_tensor(qk_ring[:, r, :].rearrange("p (v f) -> p v f", f=D), src,
                                norm[:, 3, :].unsqueeze(2).to_broadcast([P, 8, D]), ALU.mult).then_inc(s_qn, 1)

            def low(g):
                for i, buf in enumerate((q_buf, k_buf)):
                    dve.wait_ge(s_hi, 2 * g + i + 1)
                    at = bass.ds(g * IW, IW)
                    V.tensor_tensor(buf[:, 1, at], bank[:, 6 + i, :], buf[:, 0, at], ALU.subtract).then_inc(s_lo, 1)

            norms(0, 0)
            scaled(0, 0)
            with dve.Fori(0, NI // 2 - 1) as gg:
                for r in range(2):
                    g = 2 * gg + r + 1
                    norms(g, 1 - r)
                    low(g - 1)
                    scaled(g, 1 - r)
            norms(NI - 1, 1)
            low(NI - 2)
            scaled(NI - 1, 1)
            low(NI - 1)

            def mask(n, k, turn):
                dve.wait_ge(s_e, 2 * n + 2)
                dve.wait_ge(s_adj[k], 16 * (SN0 + turn + 1))
                V.scalar_tensor_tensor(p_ring[:, k, :], adj_ring[:, k, :], 0.0, p_ring[:, k, :],
                                       ALU.is_gt, ALU.mult).then_inc(s_m, 1)

            def low_part(n, k, start):
                dve.wait_ge(s_ph, n + 1)
                if not start:
                    dve.wait_ge(s_pv, n - 1)
                V.tensor_tensor(hl_buf[:, 1, k % 2, :], p_ring[:, k, :], hl_buf[:, 0, k % 2, :],
                                ALU.subtract).then_inc(s_pl, 1)

            def epilogue1(i, par):
                at = lambda step: len(EPI1) * i + EPI1.index(step) + 1
                dve.wait_ge(s_pv, RING * G1 * (i + 1))
                s = bank[:, 4 + 2 * par:6 + 2 * par, 0:2 * (D + 1)].rearrange("p b (n c) -> p b n c", n=2)[:, :, :, D]
                c4 = lambda row: den[:, row, 0:IT1]
                c22 = lambda row: c4(row).rearrange("p (b n) -> p b n", b=2)
                V.tensor_scalar(c22(1), s, 0.0, 0.5, ALU.is_gt, ALU.mult).then_inc(s_fv, 1)
                V.tensor_scalar(c22(0), s, TINY, None, ALU.max).then_inc(s_fv, 1)
                dve.wait_ge(s_fv, at("max"))
                V.reciprocal(c4(2), c4(0)).then_inc(s_fv, 1)
                dve.wait_ge(s_fv, at("recip"))
                V.tensor_tensor(c4(3), c4(2), c4(1), ALU.mult).then_inc(s_fv, 1)
                V.tensor_scalar(c4(0), c4(1), -1.0, 1.0, ALU.mult, ALU.add).then_inc(s_fv, 1)
                dve.wait_ge(s_fv, at("keep"))
                dve.wait_ge(s_fin, 32 * (i + 1))
                if not (isinstance(i, int) and i == 0):
                    dve.wait_ge(s_out, 16 * i)
                for it in range(IT1):
                    f = slice(it * P, (it + 1) * P)
                    ins = V.scalar_tensor_tensor(e_y[:, f], e_h[:, f], den[:, 0, it:it + 1], e_x1[:, f],
                                                 ALU.mult, ALU.add)
                ins.then_inc(s_fv, 1)
                dve.wait_ge(s_fv, at("kept"))
                dve.wait_ge(s_ofree, i + 1)
                V.tensor_tensor(e_y, e_y, e_t, ALU.add).then_inc(s_fv, 1)

            def chunk1(i, par):
                first = isinstance(i, int) and i == 0

                def group(g, peeled=False):
                    for k in range(RING):
                        turn = G1 * i + g
                        n = RING * turn + k
                        start = first and peeled
                        mask(n, k, turn)
                        if not (start and k == 0):
                            low_part(n - 1, (k - 1) % RING, start and k < 3)

                group(0, peeled=True)
                if not first:
                    epilogue1(i - 1, 1 - par)
                with dve.Fori(1, G1) as g:
                    group(g)

            chunks1(dve, chunk1)
            low_part(NI * RING * G1 - 1, RING - 1, False)
            epilogue1(NI - 1, 1)

        @block.tensor
        def _(pe):
            mm = nc.tensor.matmul
            pe.wait_ge(s_w, 64)
            mm(bank[:, 7, 0:2], wt_sb[:, :], a_sb[:, :], start=True, stop=True).then_inc(s_wa, 1)
            pe.wait_ge(s_ident, 2)

            def transpose(src, r, done):
                for k in range(4):
                    f = slice(k * P, (k + 1) * P)
                    ins = nc.tensor.transpose(bank[:, r, f], src[:, r, f], ident[:, :])
                ins.then_inc(done, 1)

            def t1(g, r, start=False):
                pe.wait_ge(s_h1, g + 1)
                if not start:
                    pe.wait_ge(s_h1c, g - 1)
                transpose(h_ring, r, s_h1t)

            def project(g, r, start=False):
                pe.wait_ge(s_h1c, g + 1)
                if not start:
                    pe.wait_ge(s_whc, g - 1)
                for k in range(4):
                    ins = mm(bank[:, 2 + 2 * r + k // 2, (k % 2) * VW:(k % 2 + 1) * VW],
                             ht_ring[:, r, k * P:(k + 1) * P], w_ext[:, :], start=True, stop=True)
                ins.then_inc(s_wh, 1)

            t1(0, 0, True)
            t1(1, 1, True)
            pe.wait_ge(s_wa_sb, 1)
            project(0, 0, True)
            t1(2, 0)
            project(1, 1, True)
            t1(3, 1)
            with pe.Fori(1, T // 8 - 1) as gg:
                for r in range(2):
                    project(2 * gg + r, r)
                    t1(2 * gg + r + 2, r)
            project(T // 4 - 2, 0)
            project(T // 4 - 1, 1)

            pe.wait_ge(s_ab, 1)
            nc.tensor.transpose(bank[0:T, 6, 0:P], ab_col[:, 0, :], ident[:, :]).then_inc(s_at, 1)

            pe.wait_ge(s_whc, T // 4)
            pe.wait_ge(s_const, 2)

            def chunk(c, par):
                first = isinstance(c, int) and c == 0

                def group(g, peeled=False):
                    for k in range(RING):
                        pe.wait_ge(s_p, RING * (G0 * c + g) + k + 1)
                        for jj in range(2):
                            j = 2 * (RING * g + k) + jj
                            for it in range(IT0):
                                start = peeled and k == 0 and jj == 0 and it % 3 == 0
                                f = slice((it % 4) * P, (it % 4 + 1) * P)
                                ins = mm(acc0(par, it), p0(k)[:, it // 4, jj, f], v_buf[:, bass.ds(j * VW, D + 1)],
                                         start=start, stop=False, skip_group_check=True)
                        ins.then_inc(s_used, 1)

                group(0, peeled=True)
                with pe.Fori(1, G0) as g:
                    group(g)
                if first:
                    pe.wait_ge(s_vsum, 1)
                for it in range(IT0):
                    ins = mm(acc0(par, it), empty_w[:, :], v_sum[:, :], start=False, stop=True, skip_group_check=True)
                ins.then_inc(s_acc, 1)

            chunks0(pe, chunk)

            pe.wait_ge(s_free, NC0)

            def t2(g, r, start=False):
                pe.wait_ge(s_hm[r], 8 * (g - r) + 16)
                if not start:
                    pe.wait_ge(s_htc, g - 1)
                transpose(h_ring, r, s_ht)

            def qk(g, r, start=False):
                pe.wait_ge(s_htc, g + 1)
                if not start:
                    pe.wait_ge(s_qn, g - 1)
                for k in range(4):
                    ins = mm(bank[:, 2 + 2 * r + k // 2, (k % 2) * 2 * D:(k % 2 + 1) * 2 * D],
                             ht_ring[:, r, k * P:(k + 1) * P], wqk_sb[:, :], start=True, stop=True)
                ins.then_inc(s_qk, 1)

            def t3(g, r, start=False):
                pe.wait_ge(s_qn, g + 1)
                if not start:
                    pe.wait_ge(s_lo, 2 * g)
                for k in range(4):
                    for i in range(2):
                        v = (2 * k + i) * D
                        ins = nc.tensor.transpose(bank[:, 6 + i, k * P:(k + 1) * P], qk_ring[:, r, v:v + D], ident[:, :])
                ins.then_inc(s_qt, 1)

            t2(0, 0, True)
            t2(1, 1, True)
            qk(0, 0, True)
            t2(2, 0)
            qk(1, 1, True)
            t3(0, 0, True)
            t2(3, 1)
            qk(2, 0)
            t3(1, 1)
            with pe.Fori(1, NI // 2 - 1) as gg:
                for r in range(2):
                    g = 2 * gg + r + 1
                    t2(g + 1, r)
                    qk(g, 1 - r)
                    t3(g - 1, r)
            qk(NI - 1, 1)
            t3(NI - 2, 0)
            t3(NI - 1, 1)

            pe.wait_ge(s_lo, 2 * NI)
            parts = ((0, 0), (0, 1), (1, 0))

            def scores(i, g, k, start):
                n = RING * (G1 * i + g) + k
                for hf in range(2):
                    if not start:
                        pe.wait_ge(s_e, 2 * (n - 1) + hf + 1)
                    for m in range(2):
                        j = 4 * (RING * g + k) + 2 * hf + m
                        for x, (qs, ks) in enumerate(parts):
                            ins = mm(bank[:, 2 * hf + m, :], q_buf[:, qs, bass.ds(j * P, P)],
                                     k_buf[:, ks, bass.ds(i * IW, IW)], start=(x == 0), stop=(x == 2))
                    ins.then_inc(s_s, 1)

            def values(i, q, k, par, head=False, tail=False):
                n = RING * G1 * i + q
                pe.wait_ge(s_pl, n + 1)
                for m in range(4):
                    j = 4 * q + m
                    for it in range(IT1):
                        f = slice(m * IW + it * P, m * IW + (it + 1) * P)
                        for ps, us in parts:
                            o = acc1(par, it)[:, 0:D + 1 - us]
                            v = u_buf[:, bass.ds(j, 1), us * (D + 2):us * (D + 2) + D + 1 - us]
                            ins = mm(o, hl_buf[:, ps, k % 2, f], v.rearrange("p o c -> p (o c)"),
                                     start=head and m == 0 and it % 2 == 0 and (ps, us) == (0, 0),
                                     stop=tail and m == 3 and (ps, us) == (1, 0), skip_group_check=True)
                ins.then_inc(s_pv, 1)

            def chunk1(i, par):
                first = isinstance(i, int) and i == 0
                last_q = RING * G1 - 2
                for k in range(RING):
                    scores(i, 0, k, first and k == 0)
                    if k >= 2:
                        values(i, k - 2, k - 2, par, head=(k == 2))
                    elif not first:
                        values(i - 1, last_q + k, k + 2, 1 - par, tail=(k == 1))
                with pe.Fori(1, G1) as g:
                    for k in range(RING):
                        scores(i, g, k, False)
                        values(i, RING * g + k - 2, (k - 2) % RING, par)

            chunks1(pe, chunk1)
            values(NI - 1, RING * G1 - 2, 2, 1)
            values(NI - 1, RING * G1 - 1, 3, 1, tail=True)


def kernel(x, adj, L0_gnn_W, L0_gnn_a, L1_gnn_Wq, L1_gnn_Wk):
    import concourse.bacc as bacc
    from concourse.bass_utils import run_bass_kernel_spmd

    def lanes(m):
        return np.ascontiguousarray(np.asarray(m).reshape(T, P, D).transpose(1, 0, 2).reshape(P, N))

    arrays = {
        "x": lanes(x),
        "adj": np.ascontiguousarray(np.asarray(adj).T.reshape(NJ, 2, P, NI, IW).transpose(3, 0, 2, 1, 4)
                                    .reshape(NI, NJ, P, 2 * IW)),
        "w": np.ascontiguousarray(L0_gnn_W),
        "wt": np.ascontiguousarray(np.asarray(L0_gnn_W).T),
        "a": np.ascontiguousarray(np.asarray(L0_gnn_a).reshape(2, D).T),
        "wqk": np.ascontiguousarray(np.concatenate([np.asarray(L1_gnn_Wq).T, np.asarray(L1_gnn_Wk).T], axis=1)),
    }
    nc = bacc.Bacc("TRN2", target_bir_lowering=False, num_devices=1)
    args = [nc.dram_tensor(n, v.shape, mybir.dt.from_np(v.dtype), kind="ExternalInput").ap() for n, v in arrays.items()]
    args.append(nc.dram_tensor("out", (P, N), F32, kind="ExternalOutput").ap())
    graph_layers(nc, *args)
    r = run_bass_kernel_spmd(nc, [arrays], core_ids=[0])
    got = np.asarray(r.results[0]["out"])
    return np.ascontiguousarray(got.reshape(P, T, D).transpose(1, 0, 2).reshape(N, D))
```

```python
import numpy as np
import concourse.bass as bass
from concourse import mybir
from contextlib import ExitStack

F32, F16, I32 = mybir.dt.float32, mybir.dt.float16, mybir.dt.int32
ALU = mybir.AluOpType
ACT = mybir.ActivationFunctionType
AX = mybir.AxisListType

N, D, P = 8192, 128, 128
T = N // P
IW = 512
NI = N // IW
NJ = T // 2
STEP = 2048
RING = 4
LAG = 3
C0 = 1024
NC0 = N // C0
IT0 = C0 // P
G0 = T // (STEP // C0) // RING
IT1 = IW // P
SPREAD = 6
G1 = T // (STEP // IW) // RING
VW = D + 2
UW = 2 * D + 2
EPS = 1e-5
ALPHA = 0.2
LIFT = 30.0
EMPTY = 1e-36
COS_EPS = 1e-4
UNIT = 64.0
TINY = 1e-30
LN = ("diff", "total", "m2", "dsq", "between", "var", "rstd", "nbias")
EPI0 = ("den", "neg", "elu", "x1", "stats") + LN + ("hi", "lo")
EPI1 = ("some", "max", "recip", "scale", "keep", "kept", "y")


def graph_layers(nc, x, adj, w, wt, a, wqk, out):
    ctx = ExitStack()
    with ctx:
        def sb(name, shape, dt=F32):
            return ctx.enter_context(nc.sbuf_tensor(name, shape, dt))

        def sem(name):
            return ctx.enter_context(nc.semaphore(name))

        a_rows = nc.dram_tensor("a_rows", [T, P], F32, kind="Internal").ap()
        x1_dram = nc.dram_tensor("x1_dram", [P, N], F32, kind="Internal").ap()
        h_dram = nc.dram_tensor("h_dram", [P, N], F32, kind="Internal").ap()

        ident = sb("ident", [P, P])
        a_sb = sb("a_sb", [P, 2])
        wqk_sb = sb("wqk_sb", [P, 2 * D])
        empty_w = sb("empty_w", [P, P])
        v_sum = sb("v_sum", [P, D + 1])
        stats2 = sb("stats2", [P, IT0, 6])
        small = sb("small", [P, 6, T])
        rstd = sb("rstd", [P, T])
        nbias = sb("nbias", [P, T])
        ab_col = sb("ab_col", [P, 2, T])
        ab_max = sb("ab_max", [P, 2])
        ab_top = sb("ab_top", [P, 2])
        shift = sb("shift", [P, 6])
        f_col = sb("f_col", [P, T])
        s_col = sb("s_col", [P, T])
        ns_col = sb("ns_col", [P, T])
        den = sb("den", [P, 4, IT0])
        norm = sb("norm", [P, 4, 8])

        adj_ring = sb("adj_ring", [P, RING, STEP], I32)
        p_ring = sb("p_ring", [P, RING, STEP])
        r_ring = sb("r_ring", [P, 2, C0])
        v_buf = sb("v_buf", [P, T * VW])
        q_buf = sb("q_buf", [P, 2, N], F16)
        u_buf = sb("u_buf", [P, T, UW], F16)
        hl_buf = sb("hl_buf", [P, 2, RING, STEP], F16)

        v0 = v_buf[:, :].rearrange("p (t c) -> p t c", c=VW)
        k_buf = v_buf[:, 0:N].bitcast(F16).rearrange("p (s n) -> p s n", s=2)
        xs = q_buf[:, :, :].rearrange("p s n -> p (s n)").bitcast(F32)
        scratch = hl_buf[:, :, :, :].rearrange("p s r n -> p (s r n)").bitcast(F32)
        z_buf = scratch[:, 0:C0]
        e_buf = scratch[:, C0:2 * C0]
        h_buf = scratch[:, 2 * C0:3 * C0]
        flat = p_ring[:, :, :].rearrange("p r n -> p (r n)")
        h_ring = flat[:, 0:2 * IW].rearrange("p (r n) -> p r n", r=2)
        ht_ring = flat[:, 2 * IW:4 * IW].rearrange("p (r n) -> p r n", r=2)
        sq_buf = flat[:, 4 * IW:6 * IW]
        qk_ring = flat[:, 6 * IW:10 * IW].rearrange("p (r n) -> p r n", r=2)
        w_ext = flat[:, 10 * IW:10 * IW + VW]
        wt_sb = flat[:, 11 * IW:11 * IW + P]
        at_sb = flat[0:T, 12 * IW:12 * IW + P]
        stats1 = flat[:, 13 * IW:13 * IW + 6 * T].rearrange("p (t s) -> p t s", s=6)
        e_x1 = r_ring[:, 0, 0:IW]
        e_h = r_ring[:, 0, IW:2 * IW]
        e_t = r_ring[:, 1, 0:IW]
        e_y = r_ring[:, 1, IW:2 * IW]

        bank = ctx.enter_context(nc.psum_tensor("bank", [P, 8, 512], F32))

        s_w = sem("weights_in")
        s_x = [sem(f"x_in{i}") for i in range(4)]
        s_ident = sem("ident_ready")
        s_const = sem("const_ready")
        s_wa = sem("wa_ready")
        s_wa_sb = sem("wa_copied")
        s_stats = sem("ln1_statistics")
        s_stat = sem("ln1_step")
        s_sd = sem("ln1_root")
        s_h1 = sem("h1_ready")
        s_h1t = sem("h1t_ready")
        s_h1c = sem("h1t_copied")
        s_wh = sem("wh_ready")
        s_whc = sem("wh_copied")
        s_ab = sem("ab_step")
        s_top = sem("ab_top_ready")
        s_exp0 = sem("factors_ready")
        s_at = sem("a_transposed")
        s_atc = sem("a_rows_copied")
        s_aw = sem("a_rows_written")
        s_rin = [sem("r_in0"), sem("r_in1")]
        s_r = sem("r_ready")
        s_vsum = sem("v_sum_ready")
        s_adj = [sem(f"adj_in{k}") for k in range(RING)]
        s_half = sem("relu_half")
        s_odd = sem("odd_tile_ready")
        s_even = sem("even_tile_ready")
        s_p = sem("weights_ready")
        s_used = sem("weights_used")
        s_acc = sem("layer0_sums_ready")
        s_free = sem("layer0_sums_read")
        s_ev = sem("epilogue0_vector")
        s_ea = sem("epilogue0_scalar")
        s_x1w = sem("x1_written")
        s_hw = sem("h_written")
        s_hm = [sem("h_in0"), sem("h_in1")]
        s_ht = sem("ht_ready")
        s_htc = sem("ht_copied")
        s_qk = sem("qk_ready")
        s_sq = sem("squares_ready")
        s_n2 = sem("norm_step")
        s_nr = sem("norm_root")
        s_qn = sem("qk_scaled")
        s_qt = sem("qkt_ready")
        s_hi = sem("qk_high")
        s_lo = sem("qk_low")
        s_s = sem("scores_ready")
        s_e = sem("exp_ready")
        s_m = sem("masked")
        s_ph = sem("high_ready")
        s_pl = sem("low_ready")
        s_pv = sem("layer1_used")
        s_o = sem("layer1_sums_ready")
        s_ofree = sem("layer1_sums_read")
        s_fv = sem("epilogue1_vector")
        s_fin = sem("residual_in")
        s_out = sem("out_written")

        block = ctx.enter_context(nc.Block())

        def acc0(par, it):
            b, k = 3 * par + it // 3, it % 3
            return bank[:, b, k * (D + 1):(k + 1) * (D + 1)]

        def acc0_group(par, b):
            n = min(3, IT0 - 3 * b)
            return bank[:, 3 * par + b, 0:n * (D + 1)].rearrange("p (n c) -> p n c", n=n)

        def acc1(par, it):
            return bank[:, 4 + 2 * par + it // 2, (it % 2) * (D + 1):(it % 2 + 1) * (D + 1)]

        def p0(k):
            return p_ring[:, k, :].rearrange("p (b j n) -> p b j n", b=2, j=2)

        def chunks0(eng, chunk):
            chunk(0, 0)
            with eng.Fori(0, (NC0 - 2) // 2) as pair:
                chunk(2 * pair + 1, 1)
                chunk(2 * pair + 2, 0)
            chunk(NC0 - 1, 1)

        def chunks1(eng, chunk):
            chunk(0, 0)
            with eng.Fori(0, (NI - 2) // 2) as pair:
                chunk(2 * pair + 1, 1)
                chunk(2 * pair + 2, 0)
            chunk(NI - 1, 1)

        SN0 = NC0 * G0

        @block.sync
        def _(sp):
            for i in range(4):
                q = slice(i * N // 4, (i + 1) * N // 4)
                sp.dma_start(xs[:, q], x[:, q]).then_inc(s_x[i], 16)
            sp.dma_start(w_ext[:, 0:D], w).then_inc(s_w, 16)
            sp.dma_start(wt_sb[:, :], wt).then_inc(s_w, 16)
            sp.dma_start(a_sb[:, :], a).then_inc(s_w, 16)
            sp.dma_start(wqk_sb[:, :], wqk).then_inc(s_w, 16)

            adj_lanes = adj.rearrange("b j p n -> p b j n")

            def load0(c, j, k):
                sp.dma_start(adj_ring[:, k, :].rearrange("p (b j n) -> p b j n", b=2, j=1),
                             adj_lanes[:, bass.ds(2 * c, 2), bass.ds(j, 1), :]).then_inc(s_adj[k], 16)

            def load1(i, j, k):
                sp.dma_start(adj_ring[:, k, :].rearrange("p (b j n) -> p b j n", b=1, j=2),
                             adj_lanes[:, bass.ds(i, 1), bass.ds(2 * j, 2), :]).then_inc(s_adj[k], 16)

            for k in range(RING):
                load0(0, k, k)
            sp.wait_ge(s_atc, 1)
            sp.dma_start(a_rows[:, :], at_sb[:, :]).then_inc(s_aw, 16)
            sp.wait_ge(s_aw, 16)
            a_flat = a_rows.rearrange("t p -> (t p)")

            def load_r(c, par):
                row = a_flat[bass.ds(c * C0, C0)].rearrange("(o n) -> o n", o=1)
                sp.dma_start(r_ring[:, par, :], row.to_broadcast([P, C0])).then_inc(s_rin[par], 16)

            load_r(0, 0)

            def chunk(c, par):
                first = isinstance(c, int) and c == 0
                last = isinstance(c, int) and c == NC0 - 1

                def group(g):
                    for k in range(RING):
                        sp.wait_ge(s_p, RING * (G0 * c + g - 1) + k + 1)
                        load0(c, RING * g + k, k)

                if not first:
                    group(0)
                if not last:
                    if not first:
                        sp.wait_ge(s_p, RING * G0 * c)
                    load_r(c + 1, 1 - par)
                with sp.Fori(0, G0 - 1) as h:
                    group(h + 1)

            chunks0(sp, chunk)

            sp.wait_ge(s_hw, 16 * (NC0 - 1))

            def load_h(g, r):
                sp.dma_start(h_ring[:, r, :], h_dram[:, bass.ds(g * IW, IW)]).then_inc(s_hm[r], 16)

            sp.wait_ge(s_used, RING * SN0)
            load_h(0, 0)
            load_h(1, 1)
            for k in range(RING):
                load1(0, k, k)
            with sp.Fori(0, NI // 2 - 2) as gg:
                for r in range(2):
                    sp.wait_ge(s_ht, 2 * gg + r + 1)
                    load_h(2 * gg + r + 2, r)
            sp.wait_ge(s_hw, 16 * NC0)
            for r in range(2):
                sp.wait_ge(s_ht, NI - 3 + r)
                load_h(NI - 2 + r, r)

            def chunk1(i, par):
                first = isinstance(i, int) and i == 0

                def group(g):
                    for k in range(RING):
                        sp.wait_ge(s_m, RING * (G1 * i + g - 1) + k + 1)
                        load1(i, RING * g + k, k)

                if not first:
                    group(0)
                with sp.Fori(0, G1 - 1) as h:
                    group(h + 1)

            chunks1(sp, chunk1)

        @block.gpsimd
        def _(pool):
            nc.gpsimd.memset(ident[:, :], 0.0).then_inc(s_ident, 1)
            pool.wait_ge(s_ident, 1)
            nc.gpsimd.affine_select(out=ident[:, :], in_=ident[:, :], compare_op=ALU.not_equal, fill=1.0,
                                    base=0, pattern=[[-1, P]], channel_multiplier=1).then_inc(s_ident, 1)
            nc.gpsimd.memset(empty_w[:, :], EMPTY).then_inc(s_const, 1)
            nc.gpsimd.memset(u_buf[:, :, D:D + 2], 1.0).then_inc(s_const, 1)
            pool.wait_ge(s_ab, 4)
            nc.gpsimd.partition_all_reduce(ab_top[:, :], ab_max[:, :], P, bass.bass_isa.ReduceOp.max).then_inc(s_top, 1)

        @block.scalar
        def _(act):
            act.wait_ge(s_wa, 1)
            nc.scalar.activation(w_ext[:, D:VW], bank[:, 7, 0:2], ACT.Copy).then_inc(s_wa_sb, 1)
            def norm1(g, r):
                act.nop(nofuse=True)
                for k in range(4):
                    t = 4 * g + k
                    ins = nc.scalar.activation(h_ring[:, r, k * P:(k + 1) * P], xs[:, bass.ds(t * P, P)], ACT.Relu,
                                               bias=nbias[:, bass.ds(t, 1)], scale=rstd[:, bass.ds(t, 1)])
                ins.then_inc(s_h1, 1)

            def evac1(g, r):
                act.wait_ge(s_wh, g + 1)
                act.nop(nofuse=True)
                for b in range(2):
                    src = bank[:, 2 + 2 * r + b, 0:2 * VW].rearrange("p (n c) -> p n c", n=2)
                    ins = nc.scalar.activation(v0[:, bass.ds(4 * g + 2 * b, 2), :], src, ACT.Copy)
                ins.then_inc(s_whc, 1)

            for q in range(4):
                act.wait_ge(s_stat, len(LN) * q + LN.index("var") + 1)
                nc.scalar.activation(small[:, 4, 16 * q:16 * q + 16], small[:, 3, 16 * q:16 * q + 16],
                                     ACT.Sqrt).then_inc(s_sd, 1)
                act.wait_ge(s_stat, len(LN) * (q + 1))
                if q == 0:
                    norm1(0, 0)
                    norm1(1, 1)
                with act.Fori(2 * q, 2 * q + (1 if q == 0 else 2)) as h:
                    for r in range(2):
                        g = 2 * h + r if q == 0 else 2 * h + r - 2
                        act.wait_ge(s_h1t, g + 1)
                        norm1(g + 2, r)
                        evac1(g, r)
            evac1(T // 4 - 2, 0)
            evac1(T // 4 - 1, 1)

            act.wait_ge(s_at, 1)
            nc.scalar.activation(at_sb[:, :], bank[0:T, 6, 0:P], ACT.Copy).then_inc(s_atc, 1)
            act.wait_ge(s_ab, 12)
            nc.scalar.activation(f_col[:, :], ab_col[:, 1, :], ACT.Exp, bias=shift[:, 2:3]).then_inc(s_exp0, 1)
            nc.scalar.activation(s_col[:, :], ab_col[:, 1, :], ACT.Exp, bias=shift[:, 3:4], scale=ALPHA).then_inc(s_exp0, 1)
            act.wait_ge(s_exp0, 2)
            nc.scalar.activation(ns_col[:, :], s_col[:, :], ACT.Copy, scale=-1.0).then_inc(s_exp0, 1)
            act.wait_ge(s_exp0, 3)

            def row_factor(c, par):
                act.wait_ge(s_rin[par], 16 * ((c - par) // 2 + 1) if isinstance(c, int) else 8 * (c - par) + 16)
                nc.scalar.activation(r_ring[:, par, :], r_ring[:, par, :], ACT.Exp, bias=shift[:, 4:5],
                                     scale=1.0 - ALPHA).then_inc(s_r, 1)

            row_factor(0, 0)

            def epilogue(c, par):
                at = lambda step: len(EPI0) * c + EPI0.index(step) + 1

                def quotient():
                    act.wait_ge(s_ev, at("den"))
                    for it in range(IT0):
                        ins = nc.scalar.activation(z_buf[:, it * P:(it + 1) * P], acc0(par, it)[:, 0:D], ACT.Copy,
                                                   scale=den[:, 0, it:it + 1])
                    ins.then_inc(s_free, 1)

                def exponential():
                    act.wait_ge(s_ev, at("neg"))
                    nc.scalar.activation(e_buf, e_buf, ACT.Exp).then_inc(s_ea, 1)

                def root():
                    act.wait_ge(s_ev, at("x1"))
                    act.dma_start(x1_dram[:, bass.ds(c * C0, C0)], xs[:, bass.ds(c * C0, C0)]).then_inc(s_x1w, 16)
                    act.wait_ge(s_ev, at("var"))
                    nc.scalar.activation(small[:, 4, 0:IT0], small[:, 3, 0:IT0], ACT.Sqrt).then_inc(s_ea, 1)

                def normalised():
                    act.wait_ge(s_ev, at("nbias"))
                    if not (isinstance(c, int) and c == 0):
                        act.wait_ge(s_hw, 16 * c)
                    act.nop(nofuse=True)
                    for it in range(IT0):
                        ins = nc.scalar.activation(h_buf[:, it * P:(it + 1) * P], xs[:, bass.ds(c * C0 + it * P, P)],
                                                   ACT.Relu, bias=nbias[:, it:it + 1], scale=rstd[:, it:it + 1])
                    ins.then_inc(s_ea, 1)
                    act.wait_ge(s_ea, 3 * c + 3)
                    act.dma_start(h_dram[:, bass.ds(c * C0, C0)], h_buf).then_inc(s_hw, 16)

                return quotient, exponential, root, normalised

            def chunk(c, par):
                first = isinstance(c, int) and c == 0
                last = isinstance(c, int) and c == NC0 - 1
                parts = {} if first else {(g + 1, 1): part for g, part in enumerate(epilogue(c - 1, 1 - par))}
                if not last:
                    parts[SPREAD - 1, 1] = lambda: row_factor(c + 1, 1 - par)

                def group(g, peeled=False):
                    for k in range(RING):
                        n = RING * (G0 * c + g) + k
                        j = 2 * (RING * g + k) + 1
                        if not (first and peeled):
                            act.wait_ge(s_used, n - RING + 1)
                            act.nop(nofuse=True)
                        dst = p0(k)[:, :, 1, :]
                        row = r_ring[:, par, :].rearrange("p (b n) -> p b n", b=2)
                        nc.scalar.activation(dst, row, ACT.Relu, bias=ns_col[:, bass.ds(j, 1)],
                                             scale=f_col[:, bass.ds(j, 1)]).then_inc(s_half, 1)
                        act.wait_ge(s_half, n + 1)
                        act.nop(nofuse=True)
                        nc.scalar.activation(dst, dst, ACT.Identity, bias=s_col[:, bass.ds(j, 1)]).then_inc(s_odd, 1)
                        if isinstance(g, int) and (g, k) in parts:
                            parts[g, k]()

                if first:
                    act.wait_ge(s_r, 1)
                else:
                    act.wait_ge(s_r, c + 1)
                for g in range(SPREAD):
                    group(g, peeled=(g == 0))
                with act.Fori(0, G0 - SPREAD) as h:
                    group(h + SPREAD)

            chunks0(act, chunk)
            quotient, exponential, ln_root, normalised = epilogue(NC0 - 1, 1)
            quotient()

            act.wait_ge(s_x1w, 16 * (NC0 - 1))

            def copy_ht(g, r):
                act.wait_ge(s_ht, g + 1)
                nc.scalar.activation(ht_ring[:, r, :], bank[:, r, :], ACT.Copy).then_inc(s_htc, 1)

            def square(g, r):
                act.wait_ge(s_qk, g + 1)
                nc.scalar.activation(sq_buf, bank[:, 2 + 2 * r:4 + 2 * r, :].rearrange("p b n -> p (b n)"),
                                     ACT.Square).then_inc(s_sq, 1)

            def high(g):
                act.wait_ge(s_qt, g + 1)
                act.nop(nofuse=True)
                nc.scalar.activation(q_buf[:, 0, bass.ds(g * IW, IW)], bank[:, 6, :], ACT.Copy).then_inc(s_hi, 1)
                nc.scalar.activation(k_buf[:, 0, bass.ds(g * IW, IW)], bank[:, 7, :], ACT.Copy).then_inc(s_hi, 1)

            def root(g):
                act.wait_ge(s_n2, 3 * g + 1)
                nc.scalar.activation(norm[:, 1, :], norm[:, 0, :], ACT.Sqrt).then_inc(s_nr, 1)

            def block_of(g, r):
                copy_ht(g + 1, r)
                act.wait_ge(s_n2, 3 * (g - 1) + 1)
                square(g, 1 - r)
                root(g)
                high(g - 1)

            copy_ht(0, 0)
            copy_ht(1, 1)
            exponential()
            square(0, 0)
            root(0)
            block_of(1, 0)
            ln_root()
            block_of(2, 1)
            normalised()
            block_of(3, 0)
            block_of(4, 1)
            act.wait_ge(s_x1w, 16 * NC0)
            with act.Fori(0, NI // 2 - 3) as gg:
                for r in range(2):
                    block_of(2 * gg + r + 5, r)
            act.wait_ge(s_n2, 3 * (NI - 2) + 1)
            square(NI - 1, 1)
            root(NI - 1)
            high(NI - 2)
            high(NI - 1)

            def exps(n, k):
                for hf in range(2):
                    act.wait_ge(s_s, 2 * n + hf + 1)
                    nc.scalar.activation(p_ring[:, k, hf * 1024:(hf + 1) * 1024],
                                         bank[:, 2 * hf:2 * hf + 2, :].rearrange("p b n -> p (b n)"), ACT.Exp,
                                         scale=1.0 / (UNIT * UNIT)).then_inc(s_e, 1)

            def high_part(n, k):
                act.wait_ge(s_m, n + 1)
                nc.scalar.activation(hl_buf[:, 0, k, :], p_ring[:, k, :], ACT.Copy).then_inc(s_ph, 1)

            def epilogue1(i, par):
                at = lambda step: len(EPI1) * i + EPI1.index(step) + 1

                def quotient():
                    act.wait_ge(s_fv, at("scale"))
                    for it in range(IT1):
                        ins = nc.scalar.activation(e_t[:, it * P:(it + 1) * P], acc1(par, it)[:, 0:D], ACT.Copy,
                                                   scale=den[:, 3, it:it + 1])
                    ins.then_inc(s_ofree, 1)

                def store():
                    act.wait_ge(s_fv, at("y"))
                    act.dma_start(out[:, bass.ds(i * IW, IW)], e_y).then_inc(s_out, 16)

                return quotient, store

            def residual(i):
                act.dma_start(e_x1, x1_dram[:, bass.ds(i * IW, IW)]).then_inc(s_fin, 16)
                act.dma_start(e_h, h_dram[:, bass.ds(i * IW, IW)]).then_inc(s_fin, 16)

            def chunk1(i, par):
                first = isinstance(i, int) and i == 0
                parts = {}
                if not first:
                    quotient, store = epilogue1(i - 1, 1 - par)
                    parts = {(1, 1): quotient, (2, 1): store, (2, 2): lambda: residual(i)}

                for g in range(G1):
                    for k in range(RING):
                        n = RING * (G1 * i + g) + k
                        exps(n, k)
                        if not (first and g == k == 0):
                            high_part(n - 1, (k - 1) % RING)
                        if isinstance(g, int) and (g, k) in parts:
                            parts[g, k]()

            residual(0)
            chunks1(act, chunk1)
            high_part(NI * RING * G1 - 1, RING - 1)
            for part in epilogue1(NI - 1, 1):
                part()
            act.wait_ge(s_out, 16 * NI)

        @block.vector
        def _(dve):
            V = nc.vector

            def variance(stats, lo, hi, at, done):
                me, mo = stats[:, lo:hi, 1], stats[:, lo:hi, 4]
                qe, qo = stats[:, lo:hi, 2], stats[:, lo:hi, 5]
                diff, total, sq, var = (small[:, i, lo:hi] for i in range(4))
                V.tensor_tensor(diff, me, mo, ALU.subtract).then_inc(done, 1)
                V.tensor_tensor(total, me, mo, ALU.add).then_inc(done, 1)
                V.tensor_tensor(sq, qe, qo, ALU.add).then_inc(done, 1)
                dve.wait_ge(done, at("m2"))
                V.tensor_tensor(var, diff, diff, ALU.mult).then_inc(done, 1)
                dve.wait_ge(done, at("dsq"))
                V.tensor_scalar(var, var, 0.25, EPS, ALU.mult, ALU.add).then_inc(done, 1)
                dve.wait_ge(done, at("between"))
                V.scalar_tensor_tensor(var, sq, 1.0 / D, var, ALU.mult, ALU.add).then_inc(done, 1)

            def scale_bias(lo, hi, at, done):
                V.reciprocal(rstd[:, lo:hi], small[:, 4, lo:hi]).then_inc(done, 1)
                dve.wait_ge(done, at("rstd"))
                V.scalar_tensor_tensor(nbias[:, lo:hi], small[:, 1, lo:hi], -0.5, rstd[:, lo:hi],
                                       ALU.mult, ALU.mult).then_inc(done, 1)

            def copy_h1t(g, r, start=False):
                dve.wait_ge(s_h1t, g + 1)
                if not start:
                    dve.wait_ge(s_wh, g - 1)
                V.tensor_copy(ht_ring[:, r, :], bank[:, r, :]).then_inc(s_h1c, 1)

            ln_at = lambda q: (lambda step: len(LN) * q + LN.index(step) + 1)

            def statistics(q):
                dve.wait_ge(s_x[q], 16)
                with dve.Fori(4 * q, 4 * q + 4) as g:
                    for k in range(4):
                        t = 4 * g + k
                        ins = V.bn_stats(stats1[:, bass.ds(t, 1), :].rearrange("p o s -> p (o s)"),
                                         xs[:, bass.ds(t * P, P)])
                    ins.then_inc(s_stats, 1)
                dve.wait_ge(s_stats, 4 * (q + 1))
                variance(stats1, 16 * q, 16 * q + 16, ln_at(q), s_stat)

            for q in range(4):
                statistics(q)
                dve.wait_ge(s_sd, q + 1)
                scale_bias(16 * q, 16 * q + 16, ln_at(q), s_stat)
                if q:
                    with dve.Fori(0, 2) as h:
                        for r in range(2):
                            copy_h1t(4 * q - 2 + 2 * h + r, r)
                else:
                    copy_h1t(0, 0, True)
                    copy_h1t(1, 1, True)
            copy_h1t(T // 4 - 2, 0)
            copy_h1t(T // 4 - 1, 1)

            dve.wait_ge(s_whc, T // 4)
            V.tensor_copy(ab_col[:, 0, :], v0[:, :, D]).then_inc(s_ab, 1)
            V.tensor_copy(ab_col[:, 1, :], v0[:, :, D + 1]).then_inc(s_ab, 1)
            dve.wait_ge(s_ab, 2)
            V.reduce_max(ab_max[:, 0:1], ab_col[:, 0, :], AX.X).then_inc(s_ab, 1)
            V.reduce_max(ab_max[:, 1:2], ab_col[:, 1, :], AX.X).then_inc(s_ab, 1)
            V.memset(v0[:, :, D], 1.0).then_inc(s_ab, 1)
            dve.wait_ge(s_top, 1)
            top_a, top_b = ab_top[:, 0:1], ab_top[:, 1:2]
            V.tensor_tensor(shift[:, 0:1], top_a, top_b, ALU.add).then_inc(s_ab, 1)
            V.tensor_scalar(shift[:, 2:3], top_b, -1.0, LIFT, ALU.mult, ALU.add).then_inc(s_ab, 1)
            V.tensor_scalar(shift[:, 3:4], top_b, -ALPHA, 2 * LIFT, ALU.mult, ALU.add).then_inc(s_ab, 1)
            V.tensor_scalar(shift[:, 4:5], top_b, 1.0 - ALPHA, LIFT, ALU.mult, ALU.add).then_inc(s_ab, 1)
            dve.wait_ge(s_ab, 9)
            V.tensor_scalar(shift[:, 1:2], shift[:, 0:1], 1.0 - ALPHA, 0.0, ALU.mult, ALU.max).then_inc(s_ab, 1)
            dve.wait_ge(s_ab, 10)
            V.tensor_tensor(shift[:, 3:4], shift[:, 3:4], shift[:, 1:2], ALU.subtract).then_inc(s_ab, 1)
            V.tensor_tensor(shift[:, 4:5], shift[:, 4:5], shift[:, 1:2], ALU.subtract).then_inc(s_ab, 1)

            def epilogue(c, par):
                at = lambda step: len(EPI0) * c + EPI0.index(step) + 1

                def denominators():
                    dve.wait_ge(s_acc, c + 1)
                    for b in range(3):
                        g = acc0_group(par, b)
                        ins = V.reciprocal(den[:, 0, 3 * b:3 * b + g.shape[1]], g[:, :, D])
                    ins.then_inc(s_ev, 1)

                def negative():
                    dve.wait_ge(s_free, c + 1)
                    V.tensor_scalar(e_buf, z_buf, 0.0, None, ALU.min).then_inc(s_ev, 1)

                def residual():
                    dve.wait_ge(s_ea, 3 * c + 1)
                    V.scalar_tensor_tensor(z_buf, z_buf, 0.0, e_buf, ALU.max, ALU.add).then_inc(s_ev, 1)
                    dve.wait_ge(s_ev, at("elu"))
                    x1 = xs[:, bass.ds(c * C0, C0)]
                    V.scalar_tensor_tensor(x1, z_buf, -1.0, x1, ALU.add, ALU.add).then_inc(s_ev, 1)
                    dve.wait_ge(s_ev, at("x1"))
                    dve.nop(nofuse=True)
                    for it in range(IT0):
                        ins = V.bn_stats(stats2[:, it, :], xs[:, bass.ds(c * C0 + it * P, P)])
                    ins.then_inc(s_ev, 1)
                    dve.wait_ge(s_ev, at("stats"))
                    variance(stats2, 0, IT0, at, s_ev)

                def scales():
                    dve.wait_ge(s_ea, 3 * c + 2)
                    scale_bias(0, IT0, at, s_ev)

                def split():
                    dve.wait_ge(s_ea, 3 * c + 3)
                    h8 = h_buf.rearrange("p (t f) -> p t f", f=D)
                    hi = u_buf[:, bass.ds(c * IT0, IT0), 0:D]
                    V.tensor_copy(hi, h8).then_inc(s_ev, 1)
                    dve.wait_ge(s_ev, at("hi"))
                    V.tensor_tensor(u_buf[:, bass.ds(c * IT0, IT0), D + 2:UW], h8, hi, ALU.subtract).then_inc(s_ev, 1)

                return denominators, negative, residual, scales, split

            def value_sums():
                V.reduce_sum(v_sum[:, :], v0[:, :, 0:D + 1].rearrange("p t c -> p c t"), AX.X).then_inc(s_vsum, 1)

            def chunk(c, par):
                first = isinstance(c, int) and c == 0

                parts = {} if first else {(g, RING - 1): part for g, part in enumerate(epilogue(c - 1, 1 - par))}
                if first:
                    parts[0, RING - 1] = value_sums

                def group(g, peeled=False):
                    for k in range(RING):
                        turn = G0 * c + g
                        n = RING * turn + k
                        j = 2 * (RING * g + k)
                        if not (first and peeled):
                            dve.wait_ge(s_used, n - RING + 1)
                        row = r_ring[:, par, :].rearrange("p (b n) -> p b n", b=2)
                        V.tensor_scalar(p0(k)[:, :, 0, :], row, f_col[:, bass.ds(j, 1)], s_col[:, bass.ds(j, 1)],
                                        ALU.mult, ALU.max).then_inc(s_even, 1)
                        dve.wait_ge(s_even, n + 1)
                        dve.wait_ge(s_odd, n + 1)
                        dve.wait_ge(s_adj[k], 16 * (turn + 1))
                        V.scalar_tensor_tensor(p_ring[:, k, :], adj_ring[:, k, :], 0.0, p_ring[:, k, :],
                                               ALU.is_gt, ALU.mult).then_inc(s_p, 1)
                        if isinstance(g, int) and (g, k) in parts:
                            parts[g, k]()

                dve.wait_ge(s_r, c + 1)
                if first:
                    dve.wait_ge(s_exp0, 3)
                for g in range(SPREAD):
                    group(g, peeled=(g == 0))
                with dve.Fori(0, G0 - SPREAD) as h:
                    group(h + SPREAD)

            chunks0(dve, chunk)
            denominators, negative, residual, scales, split = epilogue(NC0 - 1, 1)
            denominators()
            negative()

            def norms(g, r):
                dve.wait_ge(s_sq, g + 1)
                V.reduce_sum(norm[:, 0, :], sq_buf.rearrange("p (v f) -> p v f", f=D), AX.X).then_inc(s_n2, 1)

            def scaled(g, r, start=False):
                dve.wait_ge(s_nr, g + 1)
                if not start:
                    dve.wait_ge(s_qt, g - 1)
                V.tensor_scalar(norm[:, 2, :], norm[:, 1, :], COS_EPS, 1.0 / UNIT, ALU.max, ALU.mult).then_inc(s_n2, 1)
                dve.wait_ge(s_n2, 3 * g + 2)
                V.reciprocal(norm[:, 3, :], norm[:, 2, :]).then_inc(s_n2, 1)
                dve.wait_ge(s_n2, 3 * g + 3)
                src = bank[:, 2 + 2 * r:4 + 2 * r, :].rearrange("p b n -> p (b n)").rearrange("p (v f) -> p v f", f=D)
                V.tensor_tensor(qk_ring[:, r, :].rearrange("p (v f) -> p v f", f=D), src,
                                norm[:, 3, :].unsqueeze(2).to_broadcast([P, 8, D]), ALU.mult).then_inc(s_qn, 1)

            def low(g):
                for i, buf in enumerate((q_buf, k_buf)):
                    dve.wait_ge(s_hi, 2 * g + i + 1)
                    at = bass.ds(g * IW, IW)
                    V.tensor_tensor(buf[:, 1, at], bank[:, 6 + i, :], buf[:, 0, at], ALU.subtract).then_inc(s_lo, 1)

            def block_of(g, r, start=False):
                norms(g, 1 - r)
                scaled(g, 1 - r, start)
                low(g - 1)

            norms(0, 0)
            scaled(0, 0, True)
            residual()
            block_of(1, 0, True)
            scales()
            block_of(2, 1)
            split()
            block_of(3, 0)
            block_of(4, 1)
            with dve.Fori(0, NI // 2 - 3) as gg:
                for r in range(2):
                    block_of(2 * gg + r + 5, r)
            norms(NI - 1, 1)
            scaled(NI - 1, 1)
            low(NI - 2)
            low(NI - 1)

            def mask(n, k, turn):
                dve.wait_ge(s_e, 2 * n + 2)
                dve.wait_ge(s_adj[k], 16 * (SN0 + turn + 1))
                V.scalar_tensor_tensor(p_ring[:, k, :], adj_ring[:, k, :], 0.0, p_ring[:, k, :],
                                       ALU.is_gt, ALU.mult).then_inc(s_m, 1)

            def low_part(n, k):
                dve.wait_ge(s_ph, n + 1)
                V.tensor_tensor(hl_buf[:, 1, k, :], p_ring[:, k, :], hl_buf[:, 0, k, :],
                                ALU.subtract).then_inc(s_pl, 1)

            def epilogue1(i, par):
                at = lambda step: len(EPI1) * i + EPI1.index(step) + 1
                s = bank[:, 4 + 2 * par:6 + 2 * par, 0:2 * (D + 1)].rearrange("p b (n c) -> p b n c", n=2)[:, :, :, D]
                c4 = lambda row: den[:, row, 0:IT1]
                c22 = lambda row: c4(row).rearrange("p (b n) -> p b n", b=2)

                def factors():
                    dve.wait_ge(s_pv, RING * G1 * (i + 1))
                    V.tensor_scalar(c22(1), s, 0.0, 0.5, ALU.is_gt, ALU.mult).then_inc(s_fv, 1)
                    V.tensor_scalar(c22(0), s, TINY, None, ALU.max).then_inc(s_fv, 1)
                    dve.wait_ge(s_fv, at("max"))
                    V.reciprocal(c4(2), c4(0)).then_inc(s_fv, 1)
                    dve.wait_ge(s_fv, at("recip"))
                    V.tensor_tensor(c4(3), c4(2), c4(1), ALU.mult).then_inc(s_fv, 1)
                    V.tensor_scalar(c4(0), c4(1), -1.0, 1.0, ALU.mult, ALU.add).then_inc(s_fv, 1)

                def kept():
                    dve.wait_ge(s_fv, at("keep"))
                    dve.wait_ge(s_fin, 32 * (i + 1))
                    if not (isinstance(i, int) and i == 0):
                        dve.wait_ge(s_out, 16 * i)
                    for it in range(IT1):
                        f = slice(it * P, (it + 1) * P)
                        ins = V.scalar_tensor_tensor(e_y[:, f], e_h[:, f], den[:, 0, it:it + 1], e_x1[:, f],
                                                     ALU.mult, ALU.add)
                    ins.then_inc(s_fv, 1)

                def total():
                    dve.wait_ge(s_fv, at("kept"))
                    dve.wait_ge(s_ofree, i + 1)
                    V.tensor_tensor(e_y, e_y, e_t, ALU.add).then_inc(s_fv, 1)

                return factors, kept, total

            def chunk1(i, par):
                first = isinstance(i, int) and i == 0
                parts = {}
                if not first:
                    factors, kept, total = epilogue1(i - 1, 1 - par)
                    parts = {(0, 3): factors, (1, 1): kept, (1, 3): total}

                for g in range(G1):
                    for k in range(RING):
                        turn = G1 * i + g
                        n = RING * turn + k
                        mask(n, k, turn)
                        if not (first and g == k == 0):
                            low_part(n - 1, (k - 1) % RING)
                        if isinstance(g, int) and (g, k) in parts:
                            parts[g, k]()

            chunks1(dve, chunk1)
            low_part(NI * RING * G1 - 1, RING - 1)
            for part in epilogue1(NI - 1, 1):
                part()

        @block.tensor
        def _(pe):
            mm = nc.tensor.matmul
            pe.wait_ge(s_w, 64)
            mm(bank[:, 7, 0:2], wt_sb[:, :], a_sb[:, :], start=True, stop=True).then_inc(s_wa, 1)
            pe.wait_ge(s_ident, 2)

            def transpose(src, r, done):
                for k in range(4):
                    f = slice(k * P, (k + 1) * P)
                    ins = nc.tensor.transpose(bank[:, r, f], src[:, r, f], ident[:, :])
                ins.then_inc(done, 1)

            def t1(g, r, start=False):
                pe.wait_ge(s_h1, g + 1)
                if not start:
                    pe.wait_ge(s_h1c, g - 1)
                transpose(h_ring, r, s_h1t)

            def project(g, r, start=False):
                pe.wait_ge(s_h1c, g + 1)
                if not start:
                    pe.wait_ge(s_whc, g - 1)
                for k in range(4):
                    ins = mm(bank[:, 2 + 2 * r + k // 2, (k % 2) * VW:(k % 2 + 1) * VW],
                             ht_ring[:, r, k * P:(k + 1) * P], w_ext[:, :], start=True, stop=True)
                ins.then_inc(s_wh, 1)

            t1(0, 0, True)
            t1(1, 1, True)
            pe.wait_ge(s_wa_sb, 1)
            project(0, 0, True)
            t1(2, 0)
            project(1, 1, True)
            t1(3, 1)
            with pe.Fori(0, T // 8 - 2) as gg:
                for r in range(2):
                    project(2 * gg + r + 2, r)
                    t1(2 * gg + r + 4, r)
            project(T // 4 - 2, 0)
            project(T // 4 - 1, 1)

            pe.wait_ge(s_ab, 1)
            nc.tensor.transpose(bank[0:T, 6, 0:P], ab_col[:, 0, :], ident[:, :]).then_inc(s_at, 1)

            pe.wait_ge(s_whc, T // 4)
            pe.wait_ge(s_const, 2)

            def chunk(c, par):
                first = isinstance(c, int) and c == 0

                def group(g, peeled=False):
                    for k in range(RING):
                        pe.wait_ge(s_p, RING * (G0 * c + g) + k + 1)
                        for jj in range(2):
                            j = 2 * (RING * g + k) + jj
                            for it in range(IT0):
                                start = peeled and k == 0 and jj == 0 and it % 3 == 0
                                f = slice((it % 4) * P, (it % 4 + 1) * P)
                                ins = mm(acc0(par, it), p0(k)[:, it // 4, jj, f], v_buf[:, bass.ds(j * VW, D + 1)],
                                         start=start, stop=False, skip_group_check=True)
                        ins.then_inc(s_used, 1)

                group(0, peeled=True)
                with pe.Fori(0, G0 - 1) as h:
                    group(h + 1)
                if first:
                    pe.wait_ge(s_vsum, 1)
                for it in range(IT0):
                    ins = mm(acc0(par, it), empty_w[:, :], v_sum[:, :], start=False, stop=True, skip_group_check=True)
                ins.then_inc(s_acc, 1)

            chunks0(pe, chunk)

            def t2(g, r, start=False):
                pe.wait_ge(s_hm[r], 8 * (g - r) + 16)
                if not start:
                    pe.wait_ge(s_htc, g - 1)
                transpose(h_ring, r, s_ht)

            def qk(g, r, start=False):
                pe.wait_ge(s_htc, g + 1)
                if not start:
                    pe.wait_ge(s_qn, g - 1)
                for k in range(4):
                    ins = mm(bank[:, 2 + 2 * r + k // 2, (k % 2) * 2 * D:(k % 2 + 1) * 2 * D],
                             ht_ring[:, r, k * P:(k + 1) * P], wqk_sb[:, :], start=True, stop=True)
                ins.then_inc(s_qk, 1)

            def t3(g, r, start=False):
                pe.wait_ge(s_qn, g + 1)
                if not start:
                    pe.wait_ge(s_lo, 2 * g)
                for k in range(4):
                    for i in range(2):
                        v = (2 * k + i) * D
                        ins = nc.tensor.transpose(bank[:, 6 + i, k * P:(k + 1) * P], qk_ring[:, r, v:v + D], ident[:, :])
                ins.then_inc(s_qt, 1)

            t2(0, 0, True)
            t2(1, 1, True)
            pe.wait_ge(s_free, NC0)
            qk(0, 0, True)
            t2(2, 0)
            qk(1, 1, True)
            t3(0, 0, True)
            t2(3, 1)
            qk(2, 0)
            t3(1, 1)
            with pe.Fori(0, NI // 2 - 2) as gg:
                for r in range(2):
                    g = 2 * gg + r + 3
                    t2(g + 1, r)
                    qk(g, 1 - r)
                    t3(g - 1, r)
            qk(NI - 1, 1)
            t3(NI - 2, 0)
            t3(NI - 1, 1)

            parts = ((0, 0), (0, 1), (1, 0))

            def scores(i, g, k, start):
                n = RING * (G1 * i + g) + k
                for hf in range(2):
                    if not start:
                        pe.wait_ge(s_e, 2 * (n - 1) + hf + 1)
                    for m in range(2):
                        j = 4 * (RING * g + k) + 2 * hf + m
                        for x, (qs, ks) in enumerate(parts):
                            ins = mm(bank[:, 2 * hf + m, :], q_buf[:, qs, bass.ds(j * P, P)],
                                     k_buf[:, ks, bass.ds(i * IW, IW)], start=(x == 0), stop=(x == 2))
                    ins.then_inc(s_s, 1)

            def values(i, q, k, par, head=False, tail=False):
                n = RING * G1 * i + q
                pe.wait_ge(s_pl, n + 1)
                for m in range(4):
                    j = 4 * q + m
                    for it in range(IT1):
                        f = slice(m * IW + it * P, m * IW + (it + 1) * P)
                        for ps, us in parts:
                            o = acc1(par, it)[:, 0:D + 1 - us]
                            v = u_buf[:, bass.ds(j, 1), us * (D + 2):us * (D + 2) + D + 1 - us]
                            ins = mm(o, hl_buf[:, ps, k, f], v.rearrange("p o c -> p (o c)"),
                                     start=head and m == 0 and it % 2 == 0 and (ps, us) == (0, 0),
                                     stop=tail and m == 3 and (ps, us) == (1, 0), skip_group_check=True)
                ins.then_inc(s_pv, 1)

            def chunk1(i, par):
                first = isinstance(i, int) and i == 0
                for k in range(RING):
                    if first and k == 1:
                        pe.wait_ge(s_lo, 2 * NI)
                    scores(i, 0, k, first and k == 0)
                    if k >= LAG:
                        values(i, k - LAG, k - LAG, par, head=(k == LAG))
                    elif not first:
                        values(i - 1, RING * G1 - LAG + k, RING - LAG + k, 1 - par, tail=(k == LAG - 1))
                with pe.Fori(0, G1 - 1) as h:
                    for k in range(RING):
                        scores(i, h + 1, k, False)
                        values(i, RING * h + k + RING - LAG, (k - LAG) % RING, par)

            chunks1(pe, chunk1)
            for k in range(LAG):
                values(NI - 1, RING * G1 - LAG + k, RING - LAG + k, 1, tail=(k == LAG - 1))


def kernel(x, adj, L0_gnn_W, L0_gnn_a, L1_gnn_Wq, L1_gnn_Wk):
    import concourse.bacc as bacc
    from concourse.bass_utils import run_bass_kernel_spmd

    def lanes(m):
        return np.ascontiguousarray(np.asarray(m).reshape(T, P, D).transpose(1, 0, 2).reshape(P, N))

    arrays = {
        "x": lanes(x),
        "adj": np.ascontiguousarray(np.asarray(adj).T.reshape(NJ, 2, P, NI, IW).transpose(3, 0, 2, 1, 4)
                                    .reshape(NI, NJ, P, 2 * IW)),
        "w": np.ascontiguousarray(L0_gnn_W),
        "wt": np.ascontiguousarray(np.asarray(L0_gnn_W).T),
        "a": np.ascontiguousarray(np.asarray(L0_gnn_a).reshape(2, D).T),
        "wqk": np.ascontiguousarray(np.concatenate([np.asarray(L1_gnn_Wq).T, np.asarray(L1_gnn_Wk).T], axis=1)),
    }
    nc = bacc.Bacc("TRN2", target_bir_lowering=False, num_devices=1)
    args = [nc.dram_tensor(n, v.shape, mybir.dt.from_np(v.dtype), kind="ExternalInput").ap() for n, v in arrays.items()]
    args.append(nc.dram_tensor("out", (P, N), F32, kind="ExternalOutput").ap())
    graph_layers(nc, *args)
    r = run_bass_kernel_spmd(nc, [arrays], core_ids=[0])
    got = np.asarray(r.results[0]["out"])
    return np.ascontiguousarray(got.reshape(P, T, D).transpose(1, 0, 2).reshape(N, D))
```

```python
import numpy as np
import concourse.bass as bass
from concourse import mybir
from contextlib import ExitStack

F32, F16, I32 = mybir.dt.float32, mybir.dt.float16, mybir.dt.int32
ALU = mybir.AluOpType
ACT = mybir.ActivationFunctionType
AX = mybir.AxisListType

N, D, P = 8192, 128, 128
T = N // P
IW = 512
NI = N // IW
NJ = T // 2
STEP = 2048
RING = 4
LAG = 3
C0 = 1024
NC0 = N // C0
IT0 = C0 // P
G0 = T // (STEP // C0) // RING
IT1 = IW // P
SPREAD = 6
G1 = T // (STEP // IW) // RING
VW = D + 2
UW = 2 * D + 2
TG = T // 4
X_GROUPS = (0, 2, 4, 8, 12, TG)
LEAD = 7
EPS = 1e-5
ALPHA = 0.2
LIFT = 30.0
EMPTY = 1e-36
COS_EPS = 1e-4
VSUMS = 8
UNIT = 64.0
TINY = 1e-30
LN = ("diff", "total", "m2", "dsq", "between", "var", "rstd", "nbias")
EPI0 = ("den", "neg", "elu", "x1", "stats") + LN + ("hi", "lo")
EPI1 = ("some", "max", "recip", "scale", "keep", "kept", "y")


def graph_layers(nc, x, adj, w, wt, a, wqk, out):
    ctx = ExitStack()
    with ctx:
        def sb(name, shape, dt=F32):
            return ctx.enter_context(nc.sbuf_tensor(name, shape, dt))

        def sem(name):
            return ctx.enter_context(nc.semaphore(name))

        a_rows = nc.dram_tensor("a_rows", [T, P], F32, kind="Internal").ap()
        x1_dram = nc.dram_tensor("x1_dram", [P, N], F32, kind="Internal").ap()
        h_dram = nc.dram_tensor("h_dram", [P, N], F32, kind="Internal").ap()

        ident = sb("ident", [P, P])
        a_sb = sb("a_sb", [P, 2])
        wqk_sb = sb("wqk_sb", [P, 2 * D])
        empty_w = sb("empty_w", [P, P])
        v_sum = sb("v_sum", [P, D + 1])
        stats2 = sb("stats2", [P, IT0, 6])
        small = sb("small", [P, 6, T])
        rstd = sb("rstd", [P, T])
        nbias = sb("nbias", [P, T])
        ab_col = sb("ab_col", [P, 2, T])
        ab_max = sb("ab_max", [P, 2])
        ab_top = sb("ab_top", [P, 2])
        shift = sb("shift", [P, 6])
        f_col = sb("f_col", [P, T])
        s_col = sb("s_col", [P, T])
        ns_col = sb("ns_col", [P, T])
        den = sb("den", [P, 4, IT0])
        norm = sb("norm", [P, 4, 8])
        warm = sb("warm", [P, 1])

        adj_ring = sb("adj_ring", [P, RING, STEP], I32)
        p_ring = sb("p_ring", [P, RING, STEP])
        r_ring = sb("r_ring", [P, 2, C0])
        v_buf = sb("v_buf", [P, T * VW])
        q_buf = sb("q_buf", [P, 2, N], F16)
        u_buf = sb("u_buf", [P, T, UW], F16)
        hl_buf = sb("hl_buf", [P, 2, RING, STEP], F16)

        v0 = v_buf[:, :].rearrange("p (t c) -> p t c", c=VW)
        k_buf = v_buf[:, 0:N].bitcast(F16).rearrange("p (s n) -> p s n", s=2)
        xs = q_buf[:, :, :].rearrange("p s n -> p (s n)").bitcast(F32)
        scratch = hl_buf[:, :, :, :].rearrange("p s r n -> p (s r n)").bitcast(F32)
        z_buf = scratch[:, 0:C0]
        e_buf = scratch[:, C0:2 * C0]
        h_buf = scratch[:, 2 * C0:3 * C0]
        flat = p_ring[:, :, :].rearrange("p r n -> p (r n)")
        h_ring = scratch[:, 6 * IW:8 * IW].rearrange("p (r n) -> p r n", r=2)
        ht_ring = scratch[:, 8 * IW:10 * IW].rearrange("p (r n) -> p r n", r=2)
        sq_buf = scratch[:, 10 * IW:12 * IW]
        qk_ring = scratch[:, 12 * IW:16 * IW].rearrange("p (r n) -> p r n", r=2)
        w_ext = flat[:, 0:VW]
        wt_sb = flat[:, IW:IW + P]
        at_sb = scratch[0:T, 15 * IW:15 * IW + P]
        stats1 = flat[:, 3 * IW:3 * IW + 6 * T].rearrange("p (t s) -> p t s", s=6)
        e_x1 = r_ring[:, 0, 0:IW]
        e_h = r_ring[:, 0, IW:2 * IW]
        e_t = r_ring[:, 1, 0:IW]
        e_y = r_ring[:, 1, IW:2 * IW]

        bank = ctx.enter_context(nc.psum_tensor("bank", [P, 8, 512], F32))

        s_w = sem("weights_in")
        s_x = [sem(f"x_in{i}") for i in range(len(X_GROUPS) - 1)]
        s_ident = sem("ident_ready")
        s_const = sem("const_ready")
        s_wa = sem("wa_ready")
        s_wa_sb = sem("wa_copied")
        s_stats = sem("ln1_statistics")
        s_stat = sem("ln1_step")
        s_sd = sem("ln1_root")
        s_h1 = sem("h1_ready")
        s_h1t = sem("h1t_ready")
        s_h1c = sem("h1t_copied")
        s_wh = sem("wh_ready")
        s_whc = sem("wh_copied")
        s_ab = sem("ab_step")
        s_top = sem("ab_top_ready")
        s_exp0 = sem("factors_ready")
        s_ab0 = sem("a_broadcast")
        s_at = sem("a_transposed")
        s_atc = sem("a_rows_copied")
        s_aw = sem("a_rows_written")
        s_rin = [sem("r_in0"), sem("r_in1")]
        s_r = sem("r_ready")
        s_vsum = sem("v_sum_ready")
        s_adj = [sem(f"adj_in{k}") for k in range(RING)]
        s_half = sem("relu_half")
        s_odd = sem("odd_tile_ready")
        s_even = sem("even_tile_ready")
        s_p_first = sem("first_tile_weights_ready")
        s_p = sem("weights_ready")
        s_used = sem("weights_used")
        s_acc = sem("layer0_sums_ready")
        s_free = sem("layer0_sums_read")
        s_ev = sem("epilogue0_vector")
        s_ea = sem("epilogue0_scalar")
        s_x1w = sem("x1_written")
        s_hw = sem("h_written")
        s_hm = [sem("h_in0"), sem("h_in1")]
        s_ht = sem("ht_ready")
        s_htc = sem("ht_copied")
        s_qk = sem("qk_ready")
        s_sq = sem("squares_ready")
        s_n2 = sem("norm_step")
        s_nr = sem("norm_root")
        s_qn = sem("qk_scaled")
        s_qt = sem("qkt_ready")
        s_hi = sem("qk_high")
        s_lo = sem("qk_low")
        s_s = sem("scores_ready")
        s_e = sem("exp_ready")
        s_m = sem("masked")
        s_ph = sem("high_ready")
        s_pl = sem("low_ready")
        s_pv = sem("layer1_used")
        s_o = sem("layer1_sums_ready")
        s_ofree = sem("layer1_sums_read")
        s_fv = sem("epilogue1_vector")
        s_fin = sem("residual_in")
        s_out = sem("out_written")

        block = ctx.enter_context(nc.Block())

        def acc0(par, it):
            b, k = 3 * par + it // 3, it % 3
            return bank[:, b, k * (D + 1):(k + 1) * (D + 1)]

        def acc0_group(par, b):
            n = min(3, IT0 - 3 * b)
            return bank[:, 3 * par + b, 0:n * (D + 1)].rearrange("p (n c) -> p n c", n=n)

        def ht_bank(r):
            return bank[:, 6 + r, :]

        def qk_banks(r):
            return bank[:, 2 * r:2 * r + 2, :].rearrange("p b n -> p (b n)")

        def qkt_bank(i):
            return bank[:, 4 + i, :]

        def acc1(par, it):
            return bank[:, 4 + 2 * par + it // 2, (it % 2) * (D + 1):(it % 2 + 1) * (D + 1)]

        def p0(k):
            return p_ring[:, k, :].rearrange("p (b j n) -> p b j n", b=2, j=2)

        def chunks0(eng, chunk):
            chunk(0, 0)
            with eng.Fori(0, (NC0 - 2) // 2) as pair:
                chunk(2 * pair + 1, 1)
                chunk(2 * pair + 2, 0)
            chunk(NC0 - 1, 1)

        def chunks1(eng, chunk):
            chunk(0, 0)
            with eng.Fori(0, (NI - 2) // 2) as pair:
                chunk(2 * pair + 1, 1)
                chunk(2 * pair + 2, 0)
            chunk(NI - 1, 1)

        SN0 = NC0 * G0

        @block.sync
        def _(sp):
            def load_x(i):
                q = slice(X_GROUPS[i] * IW, X_GROUPS[i + 1] * IW)
                sp.dma_start(xs[:, q], x[:, q]).then_inc(s_x[i], 16)

            load_x(0)
            load_x(1)
            sp.dma_start(w_ext[:, 0:D], w).then_inc(s_w, 16)
            sp.dma_start(wt_sb[:, :], wt).then_inc(s_w, 16)
            sp.dma_start(a_sb[:, :], a).then_inc(s_w, 16)
            sp.dma_start(wqk_sb[:, :], wqk).then_inc(s_w, 16)
            for i in range(2, len(X_GROUPS) - 1):
                load_x(i)

            adj_lanes = adj.rearrange("b j p n -> p b j n")

            def load0(c, j, k):
                sp.dma_start(adj_ring[:, k, :].rearrange("p (b j n) -> p b j n", b=2, j=1),
                             adj_lanes[:, bass.ds(2 * c, 2), bass.ds(j, 1), :]).then_inc(s_adj[k], 16)

            def load1(i, j, k):
                sp.dma_start(adj_ring[:, k, :].rearrange("p (b j n) -> p b j n", b=1, j=2),
                             adj_lanes[:, bass.ds(i, 1), bass.ds(2 * j, 2), :]).then_inc(s_adj[k], 16)

            for k in range(RING):
                load0(0, k, k)
            sp.wait_ge(s_atc, 1)
            sp.dma_start(a_rows[:, :], at_sb[:, :]).then_inc(s_aw, 16)
            sp.wait_ge(s_aw, 16)
            a_flat = a_rows.rearrange("t p -> (t p)")

            def load_r(c, par):
                row = a_flat[bass.ds(c * C0, C0)].rearrange("(o n) -> o n", o=1)
                sp.dma_start(r_ring[:, par, :], row.to_broadcast([P, C0])).then_inc(s_rin[par], 16)

            def load_h(g, r):
                sp.dma_start(h_ring[:, r, :], h_dram[:, bass.ds(g * IW, IW)]).then_inc(s_hm[r], 16)

            def chunk(c, par):
                first = isinstance(c, int) and c == 0
                last = isinstance(c, int) and c == NC0 - 1

                def group(g):
                    for k in range(RING):
                        sp.wait_ge(s_p, RING * (G0 * c + g - 1) + k + 1)
                        load0(c, RING * g + k, k)

                if not first:
                    group(0)
                if not last:
                    if not first:
                        sp.wait_ge(s_p, RING * G0 * c)
                    load_r(c + 1, 1 - par)
                with sp.Fori(0, G0 - 2) as h:
                    group(h + 1)
                if last:
                    sp.wait_ge(s_hw, 16 * (NC0 - 1))
                    load_h(0, 0)
                    load_h(1, 1)
                group(G0 - 1)

            chunks0(sp, chunk)

            for k in range(RING):
                sp.wait_ge(s_p, RING * (SN0 - 1) + k + 1)
                load1(0, k, k)
            with sp.Fori(0, NI // 2 - 2) as gg:
                for r in range(2):
                    sp.wait_ge(s_ht, 2 * gg + r + 1)
                    load_h(2 * gg + r + 2, r)
            sp.wait_ge(s_hw, 16 * NC0)
            for r in range(2):
                sp.wait_ge(s_ht, NI - 3 + r)
                load_h(NI - 2 + r, r)

            def chunk1(i, par):
                first = isinstance(i, int) and i == 0

                def group(g):
                    for k in range(RING):
                        sp.wait_ge(s_m, RING * (G1 * i + g - 1) + k + 1)
                        load1(i, RING * g + k, k)

                if not first:
                    group(0)
                with sp.Fori(0, G1 - 1) as h:
                    group(h + 1)

            chunks1(sp, chunk1)

        @block.gpsimd
        def _(pool):
            nc.gpsimd.memset(ident[:, :], 0.0).then_inc(s_ident, 1)
            pool.wait_ge(s_ident, 1)
            nc.gpsimd.affine_select(out=ident[:, :], in_=ident[:, :], compare_op=ALU.not_equal, fill=1.0,
                                    base=0, pattern=[[-1, P]], channel_multiplier=1).then_inc(s_ident, 1)
            nc.gpsimd.memset(empty_w[:, :], EMPTY).then_inc(s_const, 1)
            nc.gpsimd.memset(u_buf[:, :, D:D + 2], 1.0).then_inc(s_const, 1)
            pool.wait_ge(s_ab, 2)
            nc.gpsimd.partition_all_reduce(ab_top[:, :], ab_max[:, :], P, bass.bass_isa.ReduceOp.max).then_inc(s_top, 1)

        @block.scalar
        def _(act):
            act.wait_ge(s_wa, 1)
            nc.scalar.activation(w_ext[:, D:VW], bank[:, 7, 0:2], ACT.Copy).then_inc(s_wa_sb, 1)

            def copy_h1t(g, start=False):
                act.wait_ge(s_h1t, g + 1)
                if not start:
                    act.wait_ge(s_wh, g - 1)
                nc.scalar.activation(ht_ring[:, g % 2, :], bank[:, g % 2, :], ACT.Relu).then_inc(s_h1c, 1)

            def evac1(g):
                act.wait_ge(s_wh, g + 1)
                for b in range(2):
                    src = bank[:, 2 + 2 * (g % 2) + b, 0:2 * VW].rearrange("p (n c) -> p n c", n=2)
                    ins = nc.scalar.activation(v0[:, 4 * g + 2 * b:4 * g + 2 * b + 2, :], src, ACT.Copy)
                ins.then_inc(s_whc, 1)

            def root1(q):
                act.wait_ge(s_stat, len(LN) * q + LN.index("var") + 1)
                nc.scalar.activation(small[:, 4, 16 * q:16 * q + 16], small[:, 3, 16 * q:16 * q + 16],
                                     ACT.Sqrt).then_inc(s_sd, 1)

            root1(0)
            copy_h1t(0, start=True)
            copy_h1t(1, start=True)
            for g in range(TG):
                evac1(g)
                if g + 2 < TG:
                    copy_h1t(g + 2)
                if g % 4 == 0 and g // 4 < 3:
                    root1(g // 4 + 1)
                if g == TG - 4:
                    act.wait_ge(s_ident, 2)
                    nc.scalar.activation(warm[:, :], ident[:, 0:1], ACT.Exp)

            act.wait_ge(s_at, 1)
            nc.scalar.activation(at_sb[:, :], bank[0:T, 5, 0:P], ACT.Copy).then_inc(s_atc, 1)
            act.wait_ge(s_ab, 12)
            nc.scalar.activation(f_col[:, :], ab_col[:, 1, :], ACT.Exp, bias=shift[:, 2:3]).then_inc(s_exp0, 1)
            nc.scalar.activation(s_col[:, :], ab_col[:, 1, :], ACT.Exp, bias=shift[:, 3:4], scale=ALPHA).then_inc(s_exp0, 1)
            act.wait_ge(s_exp0, 2)
            nc.scalar.activation(ns_col[:, :], s_col[:, :], ACT.Copy, scale=-1.0).then_inc(s_exp0, 1)
            act.wait_ge(s_exp0, 3)

            def row_factor(c, par):
                act.wait_ge(s_rin[par], 8 * c + 8 * par)
                nc.scalar.activation(r_ring[:, par, :], r_ring[:, par, :], ACT.Exp, bias=shift[:, 4:5],
                                     scale=1.0 - ALPHA).then_inc(s_r, 1)

            act.wait_ge(s_ab0, 1)
            nc.scalar.activation(r_ring[:, 0, :], bank[:, 6:8, :].rearrange("p b n -> p (b n)"), ACT.Exp,
                                 bias=shift[:, 4:5], scale=1.0 - ALPHA).then_inc(s_r, 1)

            def epilogue(c, par):
                at = lambda step: len(EPI0) * c + EPI0.index(step) + 1

                def quotient():
                    act.wait_ge(s_ev, at("den"))
                    for it in range(IT0):
                        ins = nc.scalar.activation(z_buf[:, it * P:(it + 1) * P], acc0(par, it)[:, 0:D], ACT.Copy,
                                                   scale=den[:, 0, it:it + 1])
                    ins.then_inc(s_free, 1)

                def exponential():
                    act.wait_ge(s_ev, at("neg"))
                    nc.scalar.activation(e_buf, e_buf, ACT.Exp).then_inc(s_ea, 1)

                def root():
                    act.wait_ge(s_ev, at("x1"))
                    act.dma_start(x1_dram[:, bass.ds(c * C0, C0)], xs[:, bass.ds(c * C0, C0)]).then_inc(s_x1w, 16)
                    act.wait_ge(s_ev, at("var"))
                    nc.scalar.activation(small[:, 4, 0:IT0], small[:, 3, 0:IT0], ACT.Sqrt).then_inc(s_ea, 1)

                def normalised(lo=0, hi=IT0):
                    if lo == 0:
                        act.wait_ge(s_ev, at("nbias"))
                        if not (isinstance(c, int) and c == 0):
                            act.wait_ge(s_hw, 16 * c)
                    act.nop(nofuse=True)
                    for it in range(lo, hi):
                        ins = nc.scalar.activation(h_buf[:, it * P:(it + 1) * P], xs[:, bass.ds(c * C0 + it * P, P)],
                                                   ACT.Relu, bias=nbias[:, it:it + 1], scale=rstd[:, it:it + 1])
                    if hi < IT0:
                        return
                    ins.then_inc(s_ea, 1)
                    act.wait_ge(s_ea, 3 * c + 3)
                    act.dma_start(h_dram[:, bass.ds(c * C0, C0)], h_buf).then_inc(s_hw, 16)

                return quotient, exponential, root, normalised

            def chunk(c, par):
                first = isinstance(c, int) and c == 0
                last = isinstance(c, int) and c == NC0 - 1
                parts = {} if first else {(g + 1, 1): part for g, part in enumerate(epilogue(c - 1, 1 - par))}
                if not last:
                    parts[SPREAD - 1, 1] = lambda: row_factor(c + 1, 1 - par)

                def group(g, peeled=False):
                    for k in range(RING):
                        n = RING * (G0 * c + g) + k
                        j = 2 * (RING * g + k) + 1
                        if not (first and peeled):
                            act.wait_ge(s_used, n - RING + 1)
                            act.nop(nofuse=True)
                        dst = p0(k)[:, :, 1, :]
                        row = r_ring[:, par, :].rearrange("p (b n) -> p b n", b=2)
                        nc.scalar.activation(dst, row, ACT.Relu, bias=ns_col[:, bass.ds(j, 1)],
                                             scale=f_col[:, bass.ds(j, 1)]).then_inc(s_half, 1)
                        act.wait_ge(s_half, n + 1)
                        act.nop(nofuse=True)
                        nc.scalar.activation(dst, dst, ACT.Identity, bias=s_col[:, bass.ds(j, 1)]).then_inc(s_odd, 1)
                        if isinstance(g, int) and (g, k) in parts:
                            parts[g, k]()

                if first:
                    act.wait_ge(s_r, 1)
                else:
                    act.wait_ge(s_r, c + 1)
                for g in range(SPREAD):
                    group(g, peeled=(g == 0))
                with act.Fori(0, G0 - SPREAD) as h:
                    group(h + SPREAD)

            def copy_ht(g, r):
                act.wait_ge(s_ht, g + 1)
                nc.scalar.activation(ht_ring[:, r, :], ht_bank(r), ACT.Copy).then_inc(s_htc, 1)

            chunks0(act, chunk)
            copy_ht(0, 0)
            copy_ht(1, 1)
            nc.scalar.activation(warm[:, :], ident[:, 0:1], ACT.Exp)
            quotient, exponential, ln_root, normalised = epilogue(NC0 - 1, 1)
            quotient()

            act.wait_ge(s_x1w, 16 * (NC0 - 1))

            def square(g, r):
                act.wait_ge(s_qk, g + 1)
                nc.scalar.activation(sq_buf, qk_banks(r), ACT.Square).then_inc(s_sq, 1)

            def high(g):
                act.wait_ge(s_qt, g + 1)
                act.nop(nofuse=True)
                nc.scalar.activation(q_buf[:, 0, bass.ds(g * IW, IW)], qkt_bank(0), ACT.Copy).then_inc(s_hi, 1)
                nc.scalar.activation(k_buf[:, 0, bass.ds(g * IW, IW)], qkt_bank(1), ACT.Copy).then_inc(s_hi, 1)

            def root(g):
                act.wait_ge(s_n2, 3 * g + 1)
                nc.scalar.activation(norm[:, 1, :], norm[:, 0, :], ACT.Sqrt).then_inc(s_nr, 1)

            def block_of(g, r, head=False):
                root(g)
                square(g + 1, 1 - r)
                copy_ht(g + 2, r)
                if not head:
                    high(g - 1)

            square(0, 0)
            exponential()
            block_of(0, 0, head=True)
            block_of(1, 1)
            ln_root()
            block_of(2, 0)
            for g in range(3, 7):
                block_of(g, g % 2)
                normalised(2 * (g - 3), 2 * (g - 2))
            block_of(7, 1)
            act.wait_ge(s_x1w, 16 * NC0)
            with act.Fori(0, NI // 2 - 5) as gg:
                for r in range(2):
                    block_of(2 * gg + r + 8, r)
            root(NI - 2)
            square(NI - 1, 1)
            high(NI - 3)
            root(NI - 1)

            def exps(n, k, halves=(0, 1)):
                for hf in halves:
                    act.wait_ge(s_s, 2 * n + hf + 1)
                    nc.scalar.activation(p_ring[:, k, hf * 1024:(hf + 1) * 1024],
                                         bank[:, 2 * hf:2 * hf + 2, :].rearrange("p b n -> p (b n)"), ACT.Exp,
                                         scale=1.0 / (UNIT * UNIT)).then_inc(s_e, 1)

            def high_part(n, k):
                act.wait_ge(s_m, n + 1)
                nc.scalar.activation(hl_buf[:, 0, k, :], p_ring[:, k, :], ACT.Copy).then_inc(s_ph, 1)

            def epilogue1(i, par):
                at = lambda step: len(EPI1) * i + EPI1.index(step) + 1

                def quotient():
                    act.wait_ge(s_fv, at("scale"))
                    for it in range(IT1):
                        ins = nc.scalar.activation(e_t[:, it * P:(it + 1) * P], acc1(par, it)[:, 0:D], ACT.Copy,
                                                   scale=den[:, 3, it:it + 1])
                    ins.then_inc(s_ofree, 1)

                def store():
                    act.wait_ge(s_fv, at("y"))
                    act.dma_start(out[:, bass.ds(i * IW, IW)], e_y).then_inc(s_out, 16)

                return quotient, store

            def residual(i):
                act.dma_start(e_x1, x1_dram[:, bass.ds(i * IW, IW)]).then_inc(s_fin, 16)
                act.dma_start(e_h, h_dram[:, bass.ds(i * IW, IW)]).then_inc(s_fin, 16)

            def chunk1(i, par):
                first = isinstance(i, int) and i == 0
                parts = {}
                if not first:
                    quotient, store = epilogue1(i - 1, 1 - par)
                    parts = {(1, 1): quotient, (2, 1): store, (2, 2): lambda: residual(i)}

                for g in range(G1):
                    for k in range(RING):
                        n = RING * (G1 * i + g) + k
                        if not (first and g == k == 0):
                            exps(n, k)
                        if not (first and g == k == 0):
                            high_part(n - 1, (k - 1) % RING)
                        if isinstance(g, int) and (g, k) in parts:
                            parts[g, k]()

            exps(0, 0, (0,))
            high(NI - 2)
            exps(0, 0, (1,))
            high(NI - 1)
            residual(0)
            chunks1(act, chunk1)
            high_part(NI * RING * G1 - 1, RING - 1)
            for part in epilogue1(NI - 1, 1):
                part()
            act.wait_ge(s_out, 16 * NI)

        @block.vector
        def _(dve):
            V = nc.vector

            def variance(stats, lo, hi, at, done):
                me, mo = stats[:, lo:hi, 1], stats[:, lo:hi, 4]
                qe, qo = stats[:, lo:hi, 2], stats[:, lo:hi, 5]
                diff, total, sq, var = (small[:, i, lo:hi] for i in range(4))
                V.tensor_tensor(diff, me, mo, ALU.subtract).then_inc(done, 1)
                V.tensor_tensor(total, me, mo, ALU.add).then_inc(done, 1)
                V.tensor_tensor(sq, qe, qo, ALU.add).then_inc(done, 1)
                dve.wait_ge(done, at("m2"))
                V.tensor_tensor(var, diff, diff, ALU.mult).then_inc(done, 1)
                dve.wait_ge(done, at("dsq"))
                V.tensor_scalar(var, var, 0.25, EPS, ALU.mult, ALU.add).then_inc(done, 1)
                dve.wait_ge(done, at("between"))
                V.scalar_tensor_tensor(var, sq, 1.0 / D, var, ALU.mult, ALU.add).then_inc(done, 1)

            def scale_bias(lo, hi, at, done):
                V.reciprocal(rstd[:, lo:hi], small[:, 4, lo:hi]).then_inc(done, 1)
                dve.wait_ge(done, at("rstd"))
                V.scalar_tensor_tensor(nbias[:, lo:hi], small[:, 1, lo:hi], -0.5, rstd[:, lo:hi],
                                       ALU.mult, ALU.mult).then_inc(done, 1)

            def norm1(g):
                if g >= 2:
                    dve.wait_ge(s_h1t, g - 1)
                for k in range(4):
                    t = 4 * g + k
                    ins = V.tensor_scalar(h_ring[:, g % 2, k * P:(k + 1) * P], xs[:, t * P:(t + 1) * P],
                                          rstd[:, t:t + 1], nbias[:, t:t + 1], ALU.mult, ALU.add)
                ins.then_inc(s_h1, 1)

            ln_at = lambda q: (lambda step: len(LN) * q + LN.index(step) + 1)

            def statistics(g):
                if g >= TG:
                    return
                if g in X_GROUPS:
                    dve.wait_ge(s_x[X_GROUPS.index(g)], 16)
                for t in range(4 * g, 4 * g + 4):
                    ins = V.bn_stats(stats1[:, t, :], xs[:, t * P:(t + 1) * P])
                ins.then_inc(s_stats, 1)

            def quarter_variance(q):
                dve.wait_ge(s_stats, 4 * (q + 1))
                variance(stats1, 16 * q, 16 * q + 16, ln_at(q), s_stat)

            def quarter_scales(q):
                dve.wait_ge(s_sd, q + 1)
                scale_bias(16 * q, 16 * q + 16, ln_at(q), s_stat)

            for g in range(4):
                statistics(g)
            quarter_variance(0)
            quarter_scales(0)
            dve.wait_ge(s_stat, len(LN))
            norm1(0)
            norm1(1)
            for g in range(4, LEAD):
                statistics(g)
            for g in range(TG - 2):
                q = g // 4 + 1
                if g % 4 == 2 and q < 4:
                    dve.wait_ge(s_stat, len(LN) * (q + 1))
                norm1(g + 2)
                if g % 4 == 1 and q < 4:
                    quarter_scales(q)
                statistics(g + LEAD)
                if g % 4 == 0 and q < 4:
                    quarter_variance(q)

            dve.wait_ge(s_whc, T // 4)
            V.reduce_max(ab_max[:, 0:1], v0[:, :, D], AX.X).then_inc(s_ab, 1)
            V.reduce_max(ab_max[:, 1:2], v0[:, :, D + 1], AX.X).then_inc(s_ab, 1)
            V.tensor_copy(ab_col[:, 0, :], v0[:, :, D]).then_inc(s_ab, 1)
            V.tensor_copy(ab_col[:, 1, :], v0[:, :, D + 1]).then_inc(s_ab, 1)
            dve.wait_ge(s_ab, 4)
            V.memset(v0[:, :, D], 1.0).then_inc(s_ab, 1)
            dve.wait_ge(s_top, 1)
            top_a, top_b = ab_top[:, 0:1], ab_top[:, 1:2]
            V.tensor_tensor(shift[:, 0:1], top_a, top_b, ALU.add).then_inc(s_ab, 1)
            V.tensor_scalar(shift[:, 2:3], top_b, -1.0, LIFT, ALU.mult, ALU.add).then_inc(s_ab, 1)
            V.tensor_scalar(shift[:, 3:4], top_b, -ALPHA, 2 * LIFT, ALU.mult, ALU.add).then_inc(s_ab, 1)
            V.tensor_scalar(shift[:, 4:5], top_b, 1.0 - ALPHA, LIFT, ALU.mult, ALU.add).then_inc(s_ab, 1)
            dve.wait_ge(s_ab, 9)
            V.tensor_scalar(shift[:, 1:2], shift[:, 0:1], 1.0 - ALPHA, 0.0, ALU.mult, ALU.max).then_inc(s_ab, 1)
            dve.wait_ge(s_ab, 10)
            V.tensor_tensor(shift[:, 3:4], shift[:, 3:4], shift[:, 1:2], ALU.subtract).then_inc(s_ab, 1)
            V.tensor_tensor(shift[:, 4:5], shift[:, 4:5], shift[:, 1:2], ALU.subtract).then_inc(s_ab, 1)

            def epilogue(c, par):
                at = lambda step: len(EPI0) * c + EPI0.index(step) + 1

                def denominators():
                    dve.wait_ge(s_acc, c + 1)
                    for b in range(3):
                        g = acc0_group(par, b)
                        ins = V.reciprocal(den[:, 0, 3 * b:3 * b + g.shape[1]], g[:, :, D])
                    ins.then_inc(s_ev, 1)

                def negative():
                    dve.wait_ge(s_free, c + 1)
                    V.tensor_scalar(e_buf, z_buf, 0.0, None, ALU.min).then_inc(s_ev, 1)

                def residual():
                    dve.wait_ge(s_ea, 3 * c + 1)
                    V.scalar_tensor_tensor(z_buf, z_buf, 0.0, e_buf, ALU.max, ALU.add).then_inc(s_ev, 1)
                    dve.wait_ge(s_ev, at("elu"))
                    x1 = xs[:, bass.ds(c * C0, C0)]
                    V.scalar_tensor_tensor(x1, z_buf, -1.0, x1, ALU.add, ALU.add).then_inc(s_ev, 1)

                def moments():
                    dve.wait_ge(s_ev, at("x1"))
                    dve.nop(nofuse=True)
                    for it in range(IT0):
                        ins = V.bn_stats(stats2[:, it, :], xs[:, bass.ds(c * C0 + it * P, P)])
                    ins.then_inc(s_ev, 1)
                    dve.wait_ge(s_ev, at("stats"))
                    variance(stats2, 0, IT0, at, s_ev)

                def scales():
                    dve.wait_ge(s_ea, 3 * c + 2)
                    scale_bias(0, IT0, at, s_ev)

                def split():
                    dve.wait_ge(s_ea, 3 * c + 3)
                    h8 = h_buf.rearrange("p (t f) -> p t f", f=D)
                    hi = u_buf[:, bass.ds(c * IT0, IT0), 0:D]
                    V.tensor_copy(hi, h8).then_inc(s_ev, 1)
                    dve.wait_ge(s_ev, at("hi"))
                    V.tensor_tensor(u_buf[:, bass.ds(c * IT0, IT0), D + 2:UW], h8, hi, ALU.subtract).then_inc(s_ev, 1)

                return denominators, negative, residual, moments, scales, split

            def first_masks():
                mask = adj_ring[:, 0, :].rearrange("p (b j n) -> p b j n", b=2, j=2)
                dve.wait_ge(s_adj[0], 16)
                for jj, done in enumerate((s_p_first, s_p)):
                    if jj:
                        dve.wait_ge(s_odd, 1)
                    half = p0(0)[:, :, jj, :]
                    V.scalar_tensor_tensor(half, mask[:, :, jj, :], 0.0, half, ALU.is_gt, ALU.mult).then_inc(done, 1)

            def value_sums(piece):
                cols = slice(piece * (D + 1) // VSUMS, (piece + 1) * (D + 1) // VSUMS)
                V.reduce_sum(v_sum[:, cols], v0[:, :, cols].rearrange("p t c -> p c t"), AX.X).then_inc(s_vsum, 1)

            def chunk(c, par):
                first = isinstance(c, int) and c == 0

                if not first:
                    denominators, negative, residual, moments, scales, split = epilogue(c - 1, 1 - par)
                    parts = {(0, 3): denominators, (1, 3): negative, (2, 2): residual, (2, 3): moments,
                             (3, 3): scales, (4, 3): split}
                else:
                    parts = {(i // 2, 1 + 2 * (i % 2)): (lambda i=i: value_sums(i)) for i in range(VSUMS)}

                def group(g, peeled=False):
                    for k in range(RING):
                        turn = G0 * c + g
                        n = RING * turn + k
                        j = 2 * (RING * g + k)
                        if not (first and peeled):
                            dve.wait_ge(s_used, n - RING + 1)
                        row = r_ring[:, par, :].rearrange("p (b n) -> p b n", b=2)
                        V.tensor_scalar(p0(k)[:, :, 0, :], row, f_col[:, bass.ds(j, 1)], s_col[:, bass.ds(j, 1)],
                                        ALU.mult, ALU.max).then_inc(s_even, 1)
                        dve.wait_ge(s_even, n + 1)
                        if first and peeled and k == 0:
                            first_masks()
                            continue
                        dve.wait_ge(s_odd, n + 1)
                        dve.wait_ge(s_adj[k], 16 * (turn + 1))
                        V.scalar_tensor_tensor(p_ring[:, k, :], adj_ring[:, k, :], 0.0, p_ring[:, k, :],
                                               ALU.is_gt, ALU.mult).then_inc(s_p, 1)
                        if isinstance(g, int) and (g, k) in parts:
                            parts[g, k]()

                dve.wait_ge(s_r, c + 1)
                if first:
                    dve.wait_ge(s_exp0, 3)
                for g in range(SPREAD):
                    group(g, peeled=(g == 0))
                with dve.Fori(0, G0 - SPREAD) as h:
                    group(h + SPREAD)

            chunks0(dve, chunk)
            denominators, negative, residual, moments, scales, split = epilogue(NC0 - 1, 1)
            denominators()
            negative()

            def norms(g):
                dve.wait_ge(s_sq, g + 1)
                V.reduce_sum(norm[:, 0, :], sq_buf.rearrange("p (v f) -> p v f", f=D), AX.X).then_inc(s_n2, 1)

            def scaled(g, r, start=False):
                dve.wait_ge(s_nr, g + 1)
                if not start:
                    dve.wait_ge(s_qt, g - 1)
                V.tensor_scalar(norm[:, 2, :], norm[:, 1, :], COS_EPS, 1.0 / UNIT, ALU.max, ALU.mult).then_inc(s_n2, 1)
                dve.wait_ge(s_n2, 3 * g + 2)
                V.reciprocal(norm[:, 3, :], norm[:, 2, :]).then_inc(s_n2, 1)
                dve.wait_ge(s_n2, 3 * g + 3)
                src = qk_banks(r).rearrange("p (v f) -> p v f", f=D)
                V.tensor_tensor(qk_ring[:, r, :].rearrange("p (v f) -> p v f", f=D), src,
                                norm[:, 3, :].unsqueeze(2).to_broadcast([P, 8, D]), ALU.mult).then_inc(s_qn, 1)

            def low(g):
                for i, buf in enumerate((q_buf, k_buf)):
                    dve.wait_ge(s_hi, 2 * g + i + 1)
                    at = bass.ds(g * IW, IW)
                    V.tensor_tensor(buf[:, 1, at], qkt_bank(i), buf[:, 0, at], ALU.subtract).then_inc(s_lo, 1)

            def block_of(g, r, head=False):
                norms(g)
                if not head:
                    low(g - 2)
                scaled(g, r, start=head)

            block_of(0, 0, head=True)
            residual()
            block_of(1, 1, head=True)
            moments()
            block_of(2, 0)
            scales()
            for g in range(3, 8):
                block_of(g, g % 2)
            split()
            with dve.Fori(0, NI // 2 - 4) as gg:
                for r in range(2):
                    block_of(2 * gg + r + 8, r)
            low(NI - 2)

            def mask(n, k, turn):
                dve.wait_ge(s_e, 2 * n + 2)
                dve.wait_ge(s_adj[k], 16 * (SN0 + turn + 1))
                V.scalar_tensor_tensor(p_ring[:, k, :], adj_ring[:, k, :], 0.0, p_ring[:, k, :],
                                       ALU.is_gt, ALU.mult).then_inc(s_m, 1)

            def low_part(n, k):
                dve.wait_ge(s_ph, n + 1)
                V.tensor_tensor(hl_buf[:, 1, k, :], p_ring[:, k, :], hl_buf[:, 0, k, :],
                                ALU.subtract).then_inc(s_pl, 1)

            def epilogue1(i, par):
                at = lambda step: len(EPI1) * i + EPI1.index(step) + 1
                s = bank[:, 4 + 2 * par:6 + 2 * par, 0:2 * (D + 1)].rearrange("p b (n c) -> p b n c", n=2)[:, :, :, D]
                c4 = lambda row: den[:, row, 0:IT1]
                c22 = lambda row: c4(row).rearrange("p (b n) -> p b n", b=2)

                def factors():
                    dve.wait_ge(s_pv, RING * G1 * (i + 1))
                    V.tensor_scalar(c22(1), s, 0.0, 0.5, ALU.is_gt, ALU.mult).then_inc(s_fv, 1)
                    V.tensor_scalar(c22(0), s, TINY, None, ALU.max).then_inc(s_fv, 1)
                    dve.wait_ge(s_fv, at("max"))
                    V.reciprocal(c4(2), c4(0)).then_inc(s_fv, 1)
                    dve.wait_ge(s_fv, at("recip"))
                    V.tensor_tensor(c4(3), c4(2), c4(1), ALU.mult).then_inc(s_fv, 1)
                    V.tensor_scalar(c4(0), c4(1), -1.0, 1.0, ALU.mult, ALU.add).then_inc(s_fv, 1)

                def kept():
                    dve.wait_ge(s_fv, at("keep"))
                    dve.wait_ge(s_fin, 32 * (i + 1))
                    if not (isinstance(i, int) and i == 0):
                        dve.wait_ge(s_out, 16 * i)
                    for it in range(IT1):
                        f = slice(it * P, (it + 1) * P)
                        ins = V.scalar_tensor_tensor(e_y[:, f], e_h[:, f], den[:, 0, it:it + 1], e_x1[:, f],
                                                     ALU.mult, ALU.add)
                    ins.then_inc(s_fv, 1)

                def total():
                    dve.wait_ge(s_fv, at("kept"))
                    dve.wait_ge(s_ofree, i + 1)
                    V.tensor_tensor(e_y, e_y, e_t, ALU.add).then_inc(s_fv, 1)

                return factors, kept, total

            def chunk1(i, par):
                first = isinstance(i, int) and i == 0
                parts = {}
                if not first:
                    factors, kept, total = epilogue1(i - 1, 1 - par)
                    parts = {(0, 3): factors, (1, 1): kept, (1, 3): total}

                for g in range(G1):
                    for k in range(RING):
                        turn = G1 * i + g
                        n = RING * turn + k
                        mask(n, k, turn)
                        if first and g == k == 0:
                            low(NI - 1)
                        else:
                            low_part(n - 1, (k - 1) % RING)
                        if isinstance(g, int) and (g, k) in parts:
                            parts[g, k]()

            chunks1(dve, chunk1)
            low_part(NI * RING * G1 - 1, RING - 1)
            for part in epilogue1(NI - 1, 1):
                part()

        @block.tensor
        def _(pe):
            mm = nc.tensor.matmul
            pe.wait_ge(s_w, 64)
            mm(bank[:, 7, 0:2], wt_sb[:, :], a_sb[:, :], start=True, stop=True).then_inc(s_wa, 1)
            pe.wait_ge(s_ident, 2)

            def transpose(dst, src, done):
                for k in range(4):
                    f = slice(k * P, (k + 1) * P)
                    ins = nc.tensor.transpose(dst[:, f], src[:, f], ident[:, :])
                ins.then_inc(done, 1)

            def t1(g, r, start=False):
                pe.wait_ge(s_h1, g + 1)
                if not start:
                    pe.wait_ge(s_h1c, g - 1)
                transpose(bank[:, r, :], h_ring[:, r, :], s_h1t)

            def project(g, r, start=False):
                pe.wait_ge(s_h1c, g + 1)
                if not start:
                    pe.wait_ge(s_whc, g - 1)
                for k in range(4):
                    ins = mm(bank[:, 2 + 2 * r + k // 2, (k % 2) * VW:(k % 2 + 1) * VW],
                             ht_ring[:, r, k * P:(k + 1) * P], w_ext[:, :], start=True, stop=True)
                ins.then_inc(s_wh, 1)

            t1(0, 0, True)
            t1(1, 1, True)
            pe.wait_ge(s_wa_sb, 1)
            project(0, 0, True)
            t1(2, 0)
            project(1, 1, True)
            t1(3, 1)
            with pe.Fori(0, T // 8 - 2) as gg:
                for r in range(2):
                    project(2 * gg + r + 2, r)
                    t1(2 * gg + r + 4, r)
            project(T // 4 - 2, 0)
            project(T // 4 - 1, 1)

            pe.wait_ge(s_ab, 3)
            for t in range(IT0):
                ins = nc.tensor.transpose(bank[:, 6 + t // 4, (t % 4) * P:(t % 4 + 1) * P],
                                          ab_col[:, 0, t:t + 1].to_broadcast([P, P]), ident[:, :])
            ins.then_inc(s_ab0, 1)
            nc.tensor.transpose(bank[0:T, 5, 0:P], ab_col[:, 0, :], ident[:, :]).then_inc(s_at, 1)

            pe.wait_ge(s_whc, T // 4)
            pe.wait_ge(s_const, 2)

            def t2(g, r, start=False):
                pe.wait_ge(s_hm[r], 8 * (g - r) + 16)
                if not start:
                    pe.wait_ge(s_htc, g - 1)
                transpose(ht_bank(r), h_ring[:, r, :], s_ht)

            def chunk(c, par):
                first = isinstance(c, int) and c == 0

                def group(g, peeled=False):
                    for k in range(RING):
                        split_step = first and peeled and k == 0
                        if split_step:
                            pe.wait_ge(s_p_first, 1)
                        else:
                            pe.wait_ge(s_p, RING * (G0 * c + g) + k + 1)
                        for jj in range(2):
                            if split_step and jj == 1:
                                pe.wait_ge(s_p, 1)
                            j = 2 * (RING * g + k) + jj
                            for it in range(IT0):
                                start = peeled and k == 0 and jj == 0 and it % 3 == 0
                                f = slice((it % 4) * P, (it % 4 + 1) * P)
                                ins = mm(acc0(par, it), p0(k)[:, it // 4, jj, f], v_buf[:, bass.ds(j * VW, D + 1)],
                                         start=start, stop=False, skip_group_check=True)
                        ins.then_inc(s_used, 1)

                group(0, peeled=True)
                with pe.Fori(0, G0 - 2) as h:
                    group(h + 1)
                if isinstance(c, int) and c == NC0 - 1:
                    t2(0, 0, True)
                    t2(1, 1, True)
                group(G0 - 1)
                if first:
                    pe.wait_ge(s_vsum, VSUMS)
                for it in range(IT0):
                    ins = mm(acc0(par, it), empty_w[:, :], v_sum[:, :], start=False, stop=True, skip_group_check=True)
                ins.then_inc(s_acc, 1)

            chunks0(pe, chunk)

            def qk(g, r, start=False):
                pe.wait_ge(s_htc, g + 1)
                if not start:
                    pe.wait_ge(s_qn, g - 1)
                for k in range(4):
                    ins = mm(qk_banks(r)[:, k * 2 * D:(k + 1) * 2 * D],
                             ht_ring[:, r, k * P:(k + 1) * P], wqk_sb[:, :], start=True, stop=True)
                ins.then_inc(s_qk, 1)

            def t3(g, r, start=False):
                pe.wait_ge(s_qn, g + 1)
                if not start:
                    pe.wait_ge(s_lo, 2 * g)
                for k in range(4):
                    for i in range(2):
                        v = (2 * k + i) * D
                        ins = nc.tensor.transpose(qkt_bank(i)[:, k * P:(k + 1) * P], qk_ring[:, r, v:v + D], ident[:, :])
                ins.then_inc(s_qt, 1)

            qk(0, 0, True)
            t2(2, 0)
            pe.wait_ge(s_free, NC0)
            qk(1, 1, True)
            qk(2, 0)
            t2(3, 1)
            t3(0, 0, True)
            with pe.Fori(0, NI // 2 - 2) as gg:
                for r in range(2):
                    g = 2 * gg + r + 2
                    qk(g + 1, 1 - r)
                    t2(g + 2, r)
                    t3(g - 1, 1 - r)
            qk(NI - 1, 1)
            t3(NI - 3, 1)

            parts = ((0, 0), (0, 1), (1, 0))

            def scores(i, g, k, start, halves=(0, 1)):
                n = RING * (G1 * i + g) + k
                for hf in halves:
                    if not start:
                        pe.wait_ge(s_e, 2 * (n - 1) + hf + 1)
                    for m in range(2):
                        j = 4 * (RING * g + k) + 2 * hf + m
                        for x, (qs, ks) in enumerate(parts):
                            ins = mm(bank[:, 2 * hf + m, :], q_buf[:, qs, bass.ds(j * P, P)],
                                     k_buf[:, ks, bass.ds(i * IW, IW)], start=(x == 0), stop=(x == 2))
                    ins.then_inc(s_s, 1)

            def values(i, q, k, par, head=False, tail=False):
                n = RING * G1 * i + q
                pe.wait_ge(s_pl, n + 1)
                for m in range(4):
                    j = 4 * q + m
                    for it in range(IT1):
                        f = slice(m * IW + it * P, m * IW + (it + 1) * P)
                        for ps, us in parts:
                            o = acc1(par, it)[:, 0:D + 1 - us]
                            v = u_buf[:, bass.ds(j, 1), us * (D + 2):us * (D + 2) + D + 1 - us]
                            ins = mm(o, hl_buf[:, ps, k, f], v.rearrange("p o c -> p (o c)"),
                                     start=head and m == 0 and it % 2 == 0 and (ps, us) == (0, 0),
                                     stop=tail and m == 3 and (ps, us) == (1, 0), skip_group_check=True)
                ins.then_inc(s_pv, 1)

            def chunk1(i, par):
                first = isinstance(i, int) and i == 0
                for k in range(RING):
                    if first and k == 3:
                        pe.wait_ge(s_lo, 2 * NI)
                    if not (first and k == 0):
                        scores(i, 0, k, False)
                    if k >= LAG:
                        values(i, k - LAG, k - LAG, par, head=(k == LAG))
                    elif not first:
                        values(i - 1, RING * G1 - LAG + k, RING - LAG + k, 1 - par, tail=(k == LAG - 1))
                with pe.Fori(0, G1 - 1) as h:
                    for k in range(RING):
                        scores(i, h + 1, k, False)
                        values(i, RING * h + k + RING - LAG, (k - LAG) % RING, par)

            pe.wait_ge(s_lo, 2)
            pe.wait_ge(s_qn, NI - 1)
            scores(0, 0, 0, True, (0,))
            t3(NI - 2, 0)
            pe.wait_ge(s_qn, NI)
            scores(0, 0, 0, True, (1,))
            t3(NI - 1, 1)
            chunks1(pe, chunk1)
            for k in range(LAG):
                values(NI - 1, RING * G1 - LAG + k, RING - LAG + k, 1, tail=(k == LAG - 1))


def kernel(x, adj, L0_gnn_W, L0_gnn_a, L1_gnn_Wq, L1_gnn_Wk):
    import concourse.bacc as bacc
    from concourse.bass_utils import run_bass_kernel_spmd

    def lanes(m):
        return np.ascontiguousarray(np.asarray(m).reshape(T, P, D).transpose(1, 0, 2).reshape(P, N))

    arrays = {
        "x": lanes(x),
        "adj": np.ascontiguousarray(np.asarray(adj).T.reshape(NJ, 2, P, NI, IW).transpose(3, 0, 2, 1, 4)
                                    .reshape(NI, NJ, P, 2 * IW)),
        "w": np.ascontiguousarray(L0_gnn_W),
        "wt": np.ascontiguousarray(np.asarray(L0_gnn_W).T),
        "a": np.ascontiguousarray(np.asarray(L0_gnn_a).reshape(2, D).T),
        "wqk": np.ascontiguousarray(np.concatenate([np.asarray(L1_gnn_Wq).T, np.asarray(L1_gnn_Wk).T], axis=1)),
    }
    nc = bacc.Bacc("TRN2", target_bir_lowering=False, num_devices=1)
    args = [nc.dram_tensor(n, v.shape, mybir.dt.from_np(v.dtype), kind="ExternalInput").ap() for n, v in arrays.items()]
    args.append(nc.dram_tensor("out", (P, N), F32, kind="ExternalOutput").ap())
    graph_layers(nc, *args)
    r = run_bass_kernel_spmd(nc, [arrays], core_ids=[0])
    got = np.asarray(r.results[0]["out"])
    return np.ascontiguousarray(got.reshape(P, T, D).transpose(1, 0, 2).reshape(N, D))
```
